# Optimizing a Trainium2 kernel written in Bass

```python
import numpy as np
import jax
import jax.numpy as jnp

def _softmax(x, axis=-1):
    return jax.nn.softmax(x, axis=axis)

def _gelu(x):
    return jax.nn.gelu(x, approximate=True)

def _silu(x):
    return jax.nn.silu(x)

def _sigmoid(x):
    return jax.nn.sigmoid(x)

def _layernorm(x, axis=-1, eps=1e-05):
    m = jnp.mean(x, axis=axis, keepdims=True)
    v = jnp.var(x, axis=axis, keepdims=True)
    return (x - m) / jnp.sqrt(v + eps)

def _scatter_add(tgt, idx, src, axis=0):
    return tgt.at[idx].add(src)

def _segment_sum(src, seg, n):
    return jax.ops.segment_sum(src, seg, n)
kernel_name = 'mk_prb_d1_jaxref_r8_5eaeaf'

def setup_inputs(seed: int=0):
    np.random.seed(seed)
    _w = jnp.asarray

    def _L0_attn_setup():
        import jax, jax.numpy as jnp
        import numpy as np
        B, L, D_MODEL = (2, 128, 256)
        D_INNER, D_STATE, D_CONV, DT_RANK = (512, 16, 4, 128)

        def _scan_op(c1, c2):
            a1, b1 = c1
            a2, b2 = c2
            return (a1 * a2, a2 * b1 + b2)
        key = jax.random.key(seed)
        ks = jax.random.split(key, 12)
        s_in = 1.0 / np.sqrt(D_MODEL)
        s_xp = 1.0 / np.sqrt(D_INNER)
        hidden_states = jax.random.normal(ks[0], (B, L, D_MODEL), dtype=jnp.float32)
        in_proj_w = jax.random.uniform(ks[1], (2 * D_INNER, D_MODEL), minval=-s_in, maxval=s_in)
        conv_w = jax.random.uniform(ks[2], (D_INNER, D_CONV), minval=-0.5, maxval=0.5)
        conv_b = jax.random.uniform(ks[3], (D_INNER,), minval=-0.5, maxval=0.5)
        x_proj_w = jax.random.uniform(ks[4], (DT_RANK + 2 * D_STATE, D_INNER), minval=-s_xp, maxval=s_xp)
        dt_std = DT_RANK ** (-0.5)
        dt_proj_w = jax.random.uniform(ks[5], (D_INNER, DT_RANK), minval=-dt_std, maxval=dt_std)
        dt = jnp.exp(jax.random.uniform(ks[6], (D_INNER,)) * (np.log(0.1) - np.log(0.001)) + np.log(0.001))
        dt = jnp.clip(dt, 0.0001)
        dt_proj_b = dt + jnp.log(-jnp.expm1(-dt))
        A_log = jnp.log(jnp.tile(jnp.arange(1, D_STATE + 1, dtype=jnp.float32), (D_INNER, 1)))
        D = jnp.ones((D_INNER,), dtype=jnp.float32)
        out_proj_w = jax.random.uniform(ks[7], (D_MODEL, D_INNER), minval=-s_xp, maxval=s_xp)
        return {'hidden_states': hidden_states, 'in_proj_w': in_proj_w, 'conv_w': conv_w, 'conv_b': conv_b, 'x_proj_w': x_proj_w, 'dt_proj_w': dt_proj_w, 'dt_proj_b': dt_proj_b, 'A_log': A_log, 'D': D, 'out_proj_w': out_proj_w}
    _L0_attn_in = _L0_attn_setup()

    def _L0_ffn_setup():
        import jax, jax.numpy as jnp
        import numpy as np
        NUM_EXPERTS = 64
        TOP_K = 8
        HIDDEN = 256
        INTER = 128
        key = jax.random.key(seed)
        k1, k2, k3, k4 = jax.random.split(key, 4)
        scale = 1.0 / np.sqrt(HIDDEN)
        hidden_states = jax.random.normal(k1, (4, 256, HIDDEN), dtype=jnp.float32)
        gate_w = jax.random.normal(k2, (NUM_EXPERTS, HIDDEN), dtype=jnp.float32) * scale
        w13 = jax.random.normal(k3, (NUM_EXPERTS, 2 * INTER, HIDDEN), dtype=jnp.float32) * scale
        w2 = jax.random.normal(k4, (NUM_EXPERTS, HIDDEN, INTER), dtype=jnp.float32) * (1.0 / np.sqrt(INTER))
        return {'hidden_states': hidden_states, 'gate_w': gate_w, 'w13': w13, 'w2': w2}
    _L0_ffn_in = _L0_ffn_setup()
    _d = {'L0_attn_hidden_states': _L0_attn_in['hidden_states'], 'L0_attn_in_proj_w': _L0_attn_in['in_proj_w'], 'L0_attn_conv_w': _L0_attn_in['conv_w'], 'L0_attn_conv_b': _L0_attn_in['conv_b'], 'L0_attn_x_proj_w': _L0_attn_in['x_proj_w'], 'L0_attn_dt_proj_w': _L0_attn_in['dt_proj_w'], 'L0_attn_dt_proj_b': _L0_attn_in['dt_proj_b'], 'L0_attn_A_log': _L0_attn_in['A_log'], 'L0_attn_D': _L0_attn_in['D'], 'L0_attn_out_proj_w': _L0_attn_in['out_proj_w'], 'L0_ffn_gate_w': _L0_ffn_in['gate_w'], 'L0_ffn_w13': _L0_ffn_in['w13'], 'L0_ffn_w2': _L0_ffn_in['w2']}
    _x0 = _d['L0_attn_hidden_states']
    _d['L0_attn_hidden_states'] = jax.random.normal(jax.random.fold_in(jax.random.key(seed), 1), (2, 512, 256), dtype=_x0.dtype)
    del _x0
    return _d

def reference(L0_attn_hidden_states, L0_attn_in_proj_w, L0_attn_conv_w, L0_attn_conv_b, L0_attn_x_proj_w, L0_attn_dt_proj_w, L0_attn_dt_proj_b, L0_attn_A_log, L0_attn_D, L0_attn_out_proj_w, L0_ffn_gate_w, L0_ffn_w13, L0_ffn_w2):

    def _L0_attn_ref(hidden_states, in_proj_w, conv_w, conv_b, x_proj_w, dt_proj_w, dt_proj_b, A_log, D, out_proj_w):
        import jax, jax.numpy as jnp
        import numpy as np
        B, L, D_MODEL = (2, 128, 256)
        D_INNER, D_STATE, D_CONV, DT_RANK = (512, 16, 4, 128)

        def _scan_op(c1, c2):
            a1, b1 = c1
            a2, b2 = c2
            return (a1 * a2, a2 * b1 + b2)
        d_inner = conv_w.shape[0]
        d_conv = conv_w.shape[1]
        d_state = A_log.shape[1]
        dt_rank = dt_proj_w.shape[1]
        xz = jnp.einsum('bld,ed->ble', hidden_states, in_proj_w)
        x, z = jnp.split(xz, 2, axis=-1)
        x_t = x.transpose(0, 2, 1)
        kern = conv_w[:, None, :]
        x_c = jax.lax.conv_general_dilated(x_t, kern, window_strides=(1,), padding=[(d_conv - 1, 0)], feature_group_count=d_inner)
        x = (x_c + conv_b[None, :, None]).transpose(0, 2, 1)
        x = jax.nn.silu(x)
        x_dbl = jnp.einsum('bld,ed->ble', x, x_proj_w)
        dt = x_dbl[..., :dt_rank]
        Bm = x_dbl[..., dt_rank:dt_rank + d_state]
        Cm = x_dbl[..., dt_rank + d_state:]
        dt = jnp.einsum('blr,dr->bld', dt, dt_proj_w) + dt_proj_b
        dt = jax.nn.softplus(dt + dt_proj_b)
        A = -jnp.exp(A_log)
        deltaA = jnp.exp(dt[..., None] * A)
        deltaB_u = dt[..., None] * Bm[:, :, None, :] * x[..., None]
        _, states = jax.lax.associative_scan(_scan_op, (deltaA, deltaB_u), axis=1)
        y = jnp.sum(states * Cm[:, :, None, :], axis=-1) + x * D
        y = y * z
        return jnp.einsum('bld,ed->ble', y, out_proj_w)

    def _L0_ffn_ref(hidden_states, gate_w, w13, w2):
        import jax, jax.numpy as jnp
        import numpy as np
        NUM_EXPERTS = 64
        TOP_K = 8
        HIDDEN = 256
        INTER = 128
        orig_shape = hidden_states.shape
        x = hidden_states.reshape(-1, HIDDEN)
        logits = jnp.einsum('th,eh->te', x, gate_w)
        probs = jax.nn.softmax(logits, axis=-1)
        topk_w, topk_idx = jax.lax.top_k(probs, TOP_K)
        combine = (jax.nn.one_hot(topk_idx, NUM_EXPERTS, dtype=x.dtype) * topk_w[..., None]).sum(axis=1)

        def step(acc, inp):
            w13_e, w2_e, c = inp
            g = x @ w13_e[:INTER].T
            u = x @ w13_e[INTER:].T
            h = jax.nn.silu(g) * u
            o = h @ w2_e.T
            return (acc + c[:, None] * o, None)
        out0 = jnp.zeros_like(x)
        out, _ = jax.lax.scan(step, out0, (w13, w2, combine.T))
        return out.reshape(orig_shape)
    x = L0_attn_hidden_states
    xn = _layernorm(x, axis=-1)
    x = x + _L0_attn_ref(xn, L0_attn_in_proj_w, L0_attn_conv_w, L0_attn_conv_b, L0_attn_x_proj_w, L0_attn_dt_proj_w, L0_attn_dt_proj_b, L0_attn_A_log, L0_attn_D, L0_attn_out_proj_w) + _L0_ffn_ref(xn, L0_ffn_gate_w, L0_ffn_w13, L0_ffn_w2)
    return x

_drawn_inputs = setup_inputs


def setup_inputs(seed=0):
    import zlib

    import numpy as np

    out = dict(_drawn_inputs(seed))
    spreads = {'L0_attn_D': (1.0, 0.6)}
    factors = {'L0_attn_x_proj_w': 8.0,
     'L0_attn_dt_proj_w': 8.0,
     'L0_attn_dt_proj_b': 8.0,
     'L0_attn_A_log': 8.0}
    for name, (base, spread) in spreads.items():
        noise = np.random.default_rng([zlib.crc32(name.encode()), seed]).standard_normal(out[name].shape)
        drawn = base * np.exp(spread * noise) if base else spread * noise
        out[name] = jnp.asarray(drawn.astype(out[name].dtype))
    for name, factor in factors.items():
        out[name] = (out[name] * factor).astype(out[name].dtype)
    return out
```

```python
from contextlib import ExitStack

import concourse.bass as bass
from concourse import mybir

F32 = mybir.dt.float32
I32 = mybir.dt.int32
U32 = mybir.dt.uint32
ALU = mybir.AluOpType
ACT = mybir.ActivationFunctionType
AX = mybir.AxisListType

P = 128
B, L, DM = 2, 512, 256
DI, NS, DC, R = 512, 16, 4, 128
E, K, INTER = 64, 8, 128
T = B * L
NT = T // P
KD = DM // P
DT = DI // P
G = B * DT
UNITS = G * NS
TILES = T * K // P + E
WCOL = KD * 2 * INTER + DM
EPS = 1e-5
C = 2
ATANH = (1.0, 0.33333158, 0.20012427, 0.13980709, 0.14087329)
CW, CB, DTB, DSKIP, ALOG, NPAR = 0, DC, DC + 1, DC + 2, DC + 3, DC + 3 + NS

assert UNITS == TILES == P and L == 512 and DM == 2 * P and 2 * INTER == DM


def program(nc, x, w_in, par, w_x, w_dt, w_out, w_gate, w_moe, out, bc_dram, slot_x, slot_y):
    with ExitStack() as ctx:
        def sb(name, shape, dt=F32):
            return ctx.enter_context(nc.sbuf_tensor(name, shape, dt))

        def sem(name):
            return ctx.enter_context(nc.semaphore(name))

        x_sb = sb("x_sb", [P, NT, DM])
        xT = sb("xT", [P, KD, T])
        win = sb("win", [P, KD, 2 * DI])
        xpad = sb("xpad", [P, B, DT, L + DC - 1])
        u = sb("u", [P, B, DT, L])
        dt_sb = sb("dt_sb", [P, G, L])
        dtu = sb("dtu", [P, G, L])
        bc = sb("bc", [P, NS, 2, L])
        wring = sb("wring", [P, 4, WCOL])
        prob = sb("prob", [P, NT, E])
        mask = sb("mask", [P, NT, E])
        key = sb("key", [P, NT, E])
        dbu = sb("dbu", [P, 2, L])
        hc = sb("hc", [P, 2, L])
        wx = sb("wx", [P, DT, R + 2 * NS])
        wdt = sb("wdt", [P, DI])
        wout = sb("wout", [P, DT, DM])
        wgate = sb("wgate", [P, KD, E])
        ident = sb("ident", [P, P])
        ones = sb("ones", [P, P])
        tri = sb("tri", [E, E])
        thr = sb("thr", [E, 8])
        tau = sb("tau", [E, TILES])
        pars = sb("pars", [P, DT, NPAR])
        a_neg = sb("a_neg", [P, G, NS])
        a_pos = sb("a_pos", [P, DT, NS])
        d_col = sb("d_col", [P, G, 1])
        dtb2 = sb("dtb2", [P, DT, 1])
        stats = sb("stats", [P, NT, 6])
        mv = sb("mv", [P, NT, 2])
        ve = sb("ve", [P, NT])
        sd = sb("sd", [P, NT])
        rstd = sb("rstd", [P, NT])
        mx = sb("mx", [P, NT])
        sm = sb("sm", [P, NT])
        rs = sb("rs", [P, NT])
        m8 = sb("m8", [P, NT, K])
        k8 = sb("k8", [P, NT, K])
        c8 = sb("c8", [P, NT, K])
        slot = sb("slot", [P, NT * K], U32)
        slot1 = sb("slot1", [P, NT * K], U32)
        n_tile = sb("n_tile", [E, 1])
        n_junk = sb("n_junk", [E, 8])
        base = sb("base", [E, 1])
        upto = sb("upto", [E, 1])
        tile_e = sb("tile_e", [1, TILES], I32)
        xg = sb("xg", [P, 2, 2, DM])
        xTs = sb("xTs", [P, 2, DM])
        th = sb("th", [P, 2, INTER])
        gt = sb("gt", [P, INTER])
        hh = sb("hh", [P, 2, INTER])
        ysb = sb("ysb", [P, 2, 2, DM])
        PS = [ctx.enter_context(nc.psum_tensor(f"bank{i}", [P, 512], F32)) for i in range(8)]

        zeros = bc[:, 0:2].rearrange("p a b l -> p (a b l)")
        cum = wring[0:E].rearrange("p a b -> p (a b)")[:, 0:T]
        cmp = wring[0:E].rearrange("p a b -> p (a b)")[:, T:T + TILES]
        bcs = dbu
        dtr = hc
        sp_s = xpad[:].rearrange("p b d l -> p (b d l)")[:, 0:G * L].rearrange("p (g l) -> p g l", g=G)
        sp_w = dtu
        sp_p = win[:, :, 0:DI]
        u_g = u[:].rearrange("p b d l -> p (b d) l")
        rows = bc[:].rearrange("p n c l -> p (n c l)").rearrange("p (t k d) -> p t k d", t=NT, k=K)
        match = sp_s.rearrange("p g l -> p (g l)").rearrange("p (t k e) -> p t k e", t=NT, k=K)
        Y_ACC = PS[0]
        DA = [PS[1], PS[2]]
        H = [PS[3], PS[4]]
        XT = [PS[5][:, 0:DM], PS[5][:, DM:2 * DM]]
        GU = [PS[6][:, 0:DM], PS[6][:, DM:2 * DM]]
        YT = [PS[7][:, 0:DM], PS[7][:, DM:2 * DM]]

        ld_x, ld_x1, ld_gate, ld_in, ld_par, ld_wx, ld_wdt, ld_wout = map(
            sem, "ld_x ld_x1 ld_gate ld_in ld_par ld_wx ld_wdt ld_wout".split())
        consts, zset = sem("consts"), sem("zset")
        zeroed = sem("zeroed")
        ln, sd_ready = sem("ln"), sem("sd_ready")
        xt_ps, xt_ready = sem("xt_ps"), sem("xt_ready")
        pe_r, rt, ac_r = sem("pe_r"), sem("rt"), sem("ac_r")
        in_ps, in_ready = sem("in_ps"), sem("in_ready")
        conv, u_ready = sem("conv"), sem("u_ready")
        bc_ps, bc_row, bc_st, bc_ld, bc_ld1 = map(sem, "bc_ps bc_row bc_st bc_ld bc_ld1".split())
        dr_ps, dr_ready = sem("dr_ps"), sem("dr_ready")
        dt_ps, dt_abs, dt_max = sem("dt_ps"), sem("dt_abs"), sem("dt_max")
        sp_a, sp_v, a_exp, small = sem("sp_a"), sem("sp_v"), sem("a_exp"), sem("small")
        scat, ld_res = sem("scat"), sem("ld_res")
        dA_ok, dbu_ok, scan_ok, hc_ok, acc_ok, y_out = map(
            sem, "dA_ok dbu_ok scan_ok hc_ok acc_ok y_out".split())
        xg_ld = [sem("xg_ld0"), sem("xg_ld1")]
        w_ld = [sem(f"w_ld{i}") for i in range(4)]
        y_st = [sem("y_st0"), sem("y_st1")]
        t_ok, xc_ok, gu_ok, th_ok, gt_ok, hh_ok, ye_ok, yc_ok = map(
            sem, "t_ok xc_ok gu_ok th_ok gt_ok hh_ok ye_ok yc_ok".split())
        tick = sem("tick")
        g_ld = [sem(f"g_ld{i}") for i in range(NT)]
        z_ps, z_ok, o_ps, cmb, o_st, c8_ok = map(sem, "z_ps z_ok o_ps cmb o_st c8_ok".split())

        x_t = x.rearrange("(t p) d -> p t d", p=P)
        out_t = out.rearrange("(t p) d -> p t d", p=P)
        slot_x_t = slot_x.rearrange("(i j p) d -> i p j d", j=2, p=P)
        slot_y_t = slot_y.rearrange("(i j p) d -> i p j d", j=2, p=P)
        bc_v = bc_dram.rearrange("(c n) (b l) -> b c n l", c=2, b=B)
        CONSTS = 8
        RT_SUB, RT_PROB, RT_MAX, RT_REP, RT_MASK = 2, 5, 5 + NT, 5 + 2 * NT, 6 + 2 * NT
        RT_CUM0, RT_CUM, RT_NT, RT_BASE, RT_UPTO, RT_POS, RT_CMP, RT_KEY = range(RT_MASK + 1, RT_MASK + 9)
        RT_K8 = RT_KEY + NT
        RT_SLOT, RT_SLOT1, RT_TILE = RT_K8 + 1, RT_K8 + 2, RT_K8 + 3
        block = ctx.enter_context(nc.Block())

        @block.sync
        def _(sp):
            sp.dma_start(x_sb[:, 0:NT // 2], x_t[:, 0:NT // 2]).then_inc(ld_x, 16)
            sp.dma_start(x_sb[:, NT // 2:NT], x_t[:, NT // 2:NT]).then_inc(ld_x1, 16)
            sp.dma_start(wgate[:], w_gate.rearrange("(k p) e -> p k e", p=P)).then_inc(ld_gate, 16)
            sp.dma_start(win[:], w_in.rearrange("(k p) e -> p k e", p=P)).then_inc(ld_in, 16)
            sp.dma_start(pars[:], par.rearrange("(t p) n -> p t n", p=P)).then_inc(ld_par, 16)
            sp.dma_start(wx[:], w_x.rearrange("(t p) n -> p t n", p=P)).then_inc(ld_wx, 16)
            sp.dma_start(wdt[:], w_dt).then_inc(ld_wdt, 16)
            sp.dma_start(wout[:], w_out.rearrange("(t p) n -> p t n", p=P)).then_inc(ld_wout, 16)
            sp.wait_ge(bc_row, B)
            sp.dma_start(bc_dram, bcs[0:2 * NS].rearrange("p b l -> p (b l)")).then_inc(bc_st, 16)
            sp.wait_ge(bc_st, 16)
            sp.wait_ge(zeroed, 256)
            sp.wait_ge(rt, RT_CUM)

            def spread(b, q, done):
                for c in range(2):
                    sp.dma_start(bc[:, 4 * q:4 * q + 4, c], bc_v[b, c, 4 * q:4 * q + 4].partition_broadcast(P)).then_inc(done, 16)

            for q in range(NS // 4):
                spread(0, q, bc_ld)
            sp.wait_ge(rt, RT_TILE)

            def load_w(s, j, wait=None):
                e = sp.value_load(tile_e[0:1, bass.ds(s, 1)], min_val=0, max_val=E - 1)
                if wait is not None:
                    sp.wait_ge(ye_ok, wait)
                sp.dma_start(wring[:, j], w_moe[bass.ds(e, 1)].rearrange("a p n -> p (a n)")).then_inc(w_ld[j], 16)

            def load_x(i, j):
                sp.dma_start(xg[:, j], slot_x_t[bass.ds(i, 1)].rearrange("a p j d -> p (a j) d")).then_inc(xg_ld[j], 16)

            def store_y(i, j):
                sp.dma_start(slot_y_t[bass.ds(i, 1)].rearrange("a p j d -> p (a j) d"), ysb[:, j]).then_inc(y_st[j], 16)

            for j in range(2):
                sp.sem_inc(y_st[j], 16)
            for j in range(3):
                load_w(j, j)
            sp.wait_ge(scat, 16 * NT * K)
            load_x(0, 0)
            load_x(1, 1)
            sp.dma_start(x_sb[:], x_t).then_inc(ld_res, 16)

            def quad(Q, last=False):
                load_w(4 * Q + 3, 3, 4 * Q + 2)
                if not last:
                    sp.wait_ge(t_ok, 4 * Q + 2)
                    load_x(2 * Q + 2, 0)
                    load_w(4 * Q + 4, 0, 4 * Q + 3)
                sp.wait_ge(yc_ok, 4 * Q + 2 + C)
                store_y(2 * Q, 0)
                if not last:
                    load_w(4 * Q + 5, 1, 4 * Q + 4)
                    sp.wait_ge(t_ok, 4 * Q + 4)
                    load_x(2 * Q + 3, 1)
                    load_w(4 * Q + 6, 2, 4 * Q + 5)
                sp.wait_ge(yc_ok, 4 * Q + 4 + C)
                store_y(2 * Q + 1, 1)

            GQ = NS // 4
            with sp.Fori(0, (DT - 1) * GQ) as Q:
                quad(Q)
            for q in range(GQ):
                quad((DT - 1) * GQ + q)
                sp.wait_ge(hc_ok, ((DT - 1) * GQ + q + 1) * 4 + C)
                sp.wait_ge(dbu_ok, ((DT - 1) * GQ + q + 1) * 4)
                spread(1, q, bc_ld1)
            with sp.Fori(DT * GQ, G * GQ - 1) as Q:
                quad(Q)
            quad(G * GQ - 1, last=True)
            for t in range(NT):
                sp.wait_ge(cmb, (K + 2) * (t + 1))
                sp.dma_start(out_t[:, t], x_sb[:, t]).then_inc(o_st, 16)
            sp.wait_ge(o_st, 16 * NT)

        @block.gpsimd
        def _(pool):
            nc.gpsimd.memset(zeros, 0.0).then_inc(zset, 1)
            nc.gpsimd.memset(ones[:], 1.0).then_inc(consts, 1)
            nc.gpsimd.memset(xpad[:, :, :, 0:DC - 1], 0.0).then_inc(consts, 1)
            nc.gpsimd.iota(thr[:], [[P, 8]], base=0, channel_multiplier=0,
                           allow_small_or_imprecise_dtypes=True).then_inc(consts, 1)
            nc.gpsimd.iota(tau[:], [[1, TILES]], base=0, channel_multiplier=0,
                           allow_small_or_imprecise_dtypes=True).then_inc(consts, 1)
            nc.gpsimd.memset(hh[:, 1], 0.0).then_inc(consts, 1)
            nc.gpsimd.memset(wring[:, 3, KD * 2 * INTER:], 0.0).then_inc(consts, 1)
            pool.wait_ge(consts, 6)
            nc.gpsimd.affine_select(out=ident[:], in_=ones[:], compare_op=ALU.is_equal, fill=0.0, base=0,
                                    pattern=[[-1, P]], channel_multiplier=1).then_inc(consts, 1)
            nc.gpsimd.affine_select(out=tri[:], in_=ones[0:E, 0:E], compare_op=ALU.is_gt, fill=0.0, base=0,
                                    pattern=[[1, E]], channel_multiplier=-1).then_inc(consts, 1)
            pool.wait_ge(rt, RT_SLOT)
            pool.wait_ge(zeroed, 256)
            for t in range(NT):
                for k in range(K):
                    pool.indirect_dma_start(
                        slot_x, bass.IndirectOffsetOnAxis(ap=slot[:, t * K + k:t * K + k + 1], axis=0),
                        x_sb[:, t, :], None).then_inc(scat, 16)
            pool.wait_ge(sp_v, 8 * G // 2)
            pool.wait_ge(bc_ld, 2 * 16 * (NS // 4))

            def group(g):
                with pool.Fori(0, NS // 2) as q:
                    for j in range(2):
                        s = g * NS + q * 2 + j
                        pool.wait_ge(scan_ok, s + C - 1)
                        pool.sem_inc(tick, 1)
                        nc.gpsimd.tensor_tensor(
                            dbu[:, j], dtu[:, bass.ds(g, 1)].rearrange("p a l -> p (a l)"),
                            bc[:, bass.ds(q * 2 + j, 1), 0].rearrange("p a l -> p (a l)"), ALU.mult).then_inc(dbu_ok, 1)

            with pool.Fori(0, DT) as g:
                group(g)
            pool.wait_ge(bc_ld1, 2 * 16 * (NS // 4))
            with pool.Fori(DT, G) as g:
                group(g)
            pool.wait_ge(y_st[0], 16 * (TILES // 4) + 16)
            pool.wait_ge(y_st[1], 16 * (TILES // 4) + 16)
            pool.wait_ge(hc_ok, UNITS + C)
            pool.wait_ge(dbu_ok, UNITS)
            for t in range(NT):
                for k in range(K):
                    pool.indirect_dma_start(
                        rows[:, t, k, :], None, slot_y,
                        bass.IndirectOffsetOnAxis(ap=slot1[:, t * K + k:t * K + k + 1], axis=0)).then_inc(g_ld[t], 16)

        @block.vector
        def _(dve):
            for t in range(NT):
                if t % (NT // 2) == 0:
                    dve.wait_ge([ld_x, ld_x1][t // (NT // 2)], 16)
                nc.vector.bn_stats(stats[:, t], x_sb[:, t]).then_inc(ln, 1)
            dve.wait_ge(ln, NT)
            for t in range(NT):
                nc.vector.bn_aggr(mv[:, t], stats[:, t]).then_inc(ln, 1)
            dve.wait_ge(ln, 2 * NT)
            nc.vector.tensor_scalar(ve[:], mv[:, :, 1], EPS, None, ALU.add).then_inc(ln, 1)
            dve.wait_ge(sd_ready, 1)
            nc.vector.reciprocal(rstd[:], sd[:]).then_inc(ln, 1)
            dve.wait_ge(ln, 2 * NT + 2)
            for t in range(NT):
                nc.vector.tensor_scalar(x_sb[:, t], x_sb[:, t], mv[:, t, 0:1], rstd[:, t:t + 1],
                                        ALU.subtract, ALU.mult).then_inc(ln, 1)
            for h in range(2):
                dve.wait_ge(xt_ps, 2 * h + 1)
                nc.vector.tensor_copy(xT[:, 0, h * 512:(h + 1) * 512], PS[2 * h][:]).then_inc(xt_ready, 1)
            logit = PS[4][:].rearrange("p (t e) -> p t e", t=NT)
            dve.wait_ge(pe_r, 1)
            nc.vector.tensor_reduce(mx[:], logit, AX.X, ALU.max).then_inc(rt, 1)
            dve.wait_ge(rt, 1)
            nc.vector.tensor_tensor(prob[:], logit, mx[:].unsqueeze(2).broadcast_to([P, NT, E]), ALU.subtract).then_inc(rt, 1)
            dve.wait_ge(ac_r, 1)
            nc.vector.tensor_reduce(sm[:], prob[:], AX.X, ALU.add).then_inc(rt, 1)
            dve.wait_ge(rt, 3)
            nc.vector.reciprocal(rs[:], sm[:]).then_inc(rt, 1)
            dve.wait_ge(rt, 4)
            nc.vector.tensor_tensor(prob[:], prob[:], rs[:].unsqueeze(2).broadcast_to([P, NT, E]), ALU.mult).then_inc(rt, 1)
            dve.wait_ge(rt, RT_PROB)
            for t in range(NT):
                nc.vector.max(m8[:, t], prob[:, t]).then_inc(rt, 1)
            dve.wait_ge(rt, RT_MAX)
            for t in range(NT):
                nc.vector.match_replace(mask[:, t], m8[:, t], prob[:, t], -1.0).then_inc(rt, 1)
            dve.wait_ge(rt, RT_REP)
            nc.vector.tensor_scalar(mask[:], mask[:], 0.0, None, ALU.is_lt).then_inc(rt, 1)

            def conv_block(d):
                dve.wait_ge(in_ready, 2 * d + 2)
                tap = lambda j: pars[:, d, CW + j:CW + j + 1]
                nc.vector.tensor_scalar(u[:, :, d], xpad[:, :, d, 0:L], tap(0), None, ALU.mult).then_inc(conv, 1)
                for j in range(1, DC):
                    dve.wait_ge(conv, DC * d + j)
                    nc.vector.scalar_tensor_tensor(u[:, :, d], xpad[:, :, d, j:j + L], tap(j), u[:, :, d],
                                                   ALU.mult, ALU.add).then_inc(conv, 1)

            dve.wait_ge(ld_par, 16)
            dve.wait_ge(consts, CONSTS)
            conv_block(0)
            conv_block(1)
            dve.wait_ge(pe_r, 2)
            dve.wait_ge(zset, 1)
            zrow = zeros[0:E, 0:512]
            nc.vector.tensor_tensor_scan(cum[:, 0:512], zrow, PS[5][0:E, :], 0.0, ALU.add, ALU.add).then_inc(rt, 1)
            dve.wait_ge(rt, RT_CUM0)
            nc.vector.tensor_tensor_scan(cum[:, 512:1024], zrow, PS[6][0:E, :], cum[:, 511:512], ALU.add, ALU.add).then_inc(rt, 1)
            dve.wait_ge(rt, RT_CUM)
            nc.vector.tensor_scalar(n_junk[:], thr[:], cum[:, T - 1:T], None, ALU.is_lt, ALU.add,
                                    accum_out=n_tile[:]).then_inc(rt, 1)
            dve.wait_ge(pe_r, 3)
            nc.vector.tensor_scalar(base[:], PS[4][0:E, 0:1], float(P), None, ALU.mult).then_inc(rt, 1)
            dve.wait_ge(rt, RT_NT)
            nc.vector.tensor_tensor(upto[:], PS[4][0:E, 0:1], n_tile[:], ALU.add).then_inc(rt, 1)
            dve.wait_ge(rt, RT_BASE)
            nc.vector.tensor_scalar(cum, cum, base[:], None, ALU.add).then_inc(rt, 1)
            dve.wait_ge(rt, RT_UPTO)
            nc.vector.tensor_scalar(cmp, tau[:], upto[:], None, ALU.is_ge).then_inc(rt, 1)
            dve.wait_ge(pe_r, 4)
            nc.vector.tensor_tensor(key[:].rearrange("p t e -> p (t e)"), mask[:].rearrange("p t e -> p (t e)"),
                                    PS[7][:], ALU.mult).then_inc(rt, 1)
            dve.wait_ge(rt, RT_KEY)
            for t in range(NT):
                nc.vector.max(k8[:, t], key[:, t]).then_inc(rt, 1)
            dve.wait_ge(rt, RT_K8)
            k8f = k8[:].rearrange("p t k -> p (t k)")
            nc.vector.tensor_scalar(slot[:], k8f, -1.0, None, ALU.add).then_inc(rt, 1)
            nc.vector.tensor_scalar(slot1[:], k8f, float(P - 1), None, ALU.add).then_inc(rt, 1)
            dve.wait_ge(pe_r, 5)
            nc.vector.tensor_scalar(tile_e[:], PS[4][0:1, P:P + TILES], float(E - 1), None, ALU.min).then_inc(rt, 1)
            conv_block(2)
            conv_block(3)
            dve.wait_ge(a_exp, 1)
            for b in range(B):
                nc.vector.tensor_scalar(a_neg[:, b * DT:(b + 1) * DT], a_pos[:], -1.0, None, ALU.mult).then_inc(small, 1)
                nc.vector.tensor_copy(d_col[:, b * DT:(b + 1) * DT], pars[:, :, DSKIP:DSKIP + 1]).then_inc(small, 1)
            nc.vector.tensor_scalar(dtb2[:], pars[:, :, DTB:DTB + 1], 2.0, None, ALU.mult).then_inc(small, 1)
            dve.wait_ge(small, 5)

            def fraction(c):
                for g in (2 * c, 2 * c + 1):
                    dve.wait_ge(dt_abs, g + 1)
                    nc.vector.tensor_scalar(dt_sb[:, g], PS[4 + g % 4][:], dtb2[:, g % DT], 0.0, ALU.add, ALU.max).then_inc(dt_max, 1)
                two = slice(2 * c, 2 * c + 2)
                dve.wait_ge(sp_a, 4 * c + 2)
                nc.vector.reciprocal(sp_w[:, two], sp_w[:, two]).then_inc(sp_v, 1)
                dve.wait_ge(sp_v, 8 * c + 1)
                nc.vector.tensor_tensor(sp_s[:, two], sp_s[:, two], sp_w[:, two], ALU.mult).then_inc(sp_v, 1)
                dve.wait_ge(sp_a, 4 * c + 4)
                nc.vector.tensor_tensor(sp_p, sp_p, sp_w[:, two], ALU.mult).then_inc(sp_v, 1)
                for n, a in enumerate((ATANH[2], ATANH[1])):
                    dve.wait_ge(sp_v, 8 * c + 3 + n)
                    nc.vector.scalar_tensor_tensor(sp_p, sp_p, a, sp_w[:, two], ALU.add, ALU.mult).then_inc(sp_v, 1)
                dve.wait_ge(sp_v, 8 * c + 5)
                nc.vector.scalar_tensor_tensor(sp_p, sp_p, ATANH[0], sp_s[:, two], ALU.add, ALU.mult).then_inc(sp_v, 1)
                dve.wait_ge(sp_v, 8 * c + 6)
                dve.wait_ge(dt_max, 2 * c + 2)
                nc.vector.scalar_tensor_tensor(dt_sb[:, two], sp_p, 2.0, dt_sb[:, two], ALU.mult, ALU.add).then_inc(sp_v, 1)
                dve.wait_ge(sp_v, 8 * c + 7)
                nc.vector.tensor_tensor(dtu[:, two], dt_sb[:, two], u_g[:, two], ALU.mult).then_inc(sp_v, 1)

            for c in range(G // 2):
                fraction(c)
            dve.wait_ge(sp_v, 8 * G // 2)
            for s_ in (scan_ok, hc_ok, hh_ok, gt_ok):
                dve.sem_inc(s_, C)
            dve.sem_inc(y_out, 1)

            def group(g):
                with dve.Fori(0, NS // 2) as q:
                    for j in range(2):
                        s = g * NS + q * 2 + j
                        n = q * 2 + j
                        dve.wait_ge(dA_ok, s + 1)
                        dve.wait_ge(dbu_ok, s + 1)
                        dve.wait_ge(hc_ok, s + C - 1)
                        nc.vector.tensor_tensor_scan(H[j][:], DA[j][:], dbu[:, j], 0.0, ALU.mult, ALU.add).then_inc(scan_ok, 1)
                        dve.wait_ge(acc_ok, s + C - 1)
                        dve.wait_ge(scan_ok, s + C + 1)
                        nc.vector.tensor_tensor(hc[:, j], H[j][:], bc[:, bass.ds(n, 1), 1].rearrange("p a l -> p (a l)"),
                                                ALU.mult).then_inc(hc_ok, 1)
                        dve.wait_ge(th_ok, s + 1)
                        dve.wait_ge(hh_ok, s + C)
                        nc.vector.scalar_tensor_tensor(gt[:], th[:, j], 1.0, GU[j][:, 0:INTER], ALU.add, ALU.mult).then_inc(gt_ok, 1)
                        dve.wait_ge(ye_ok, s + 1)
                        dve.wait_ge(gt_ok, s + C + 1)
                        nc.vector.scalar_tensor_tensor(hh[:, j], gt[:], 0.5, GU[j][:, INTER:2 * INTER], ALU.mult, ALU.mult).then_inc(hh_ok, 1)
                dve.wait_ge(acc_ok, (g + 1) * NS + C)
                ug = u_g[:, bass.ds(g, 1)].rearrange("p a l -> p (a l)")
                nc.vector.scalar_tensor_tensor(ug, ug, d_col[:, bass.ds(g, 1)].rearrange("p a l -> p (a l)"), Y_ACC[:],
                                               ALU.mult, ALU.add).then_inc(y_out, 1)

            with dve.Fori(0, G) as g:
                group(g)
            kb = key[:].unsqueeze(2).broadcast_to([P, NT, K, E])
            nc.vector.tensor_tensor(match, kb, k8[:].unsqueeze(3).broadcast_to([P, NT, K, E]), ALU.is_equal).then_inc(c8_ok, 1)
            dve.wait_ge(c8_ok, 1)
            nc.vector.tensor_tensor(match, match, prob[:].unsqueeze(2).broadcast_to([P, NT, K, E]), ALU.mult).then_inc(c8_ok, 1)
            dve.wait_ge(c8_ok, 2)
            nc.vector.tensor_reduce(c8[:], match, AX.X, ALU.add).then_inc(c8_ok, 1)
            dve.wait_ge(y_out, G + 1)
            for g in range(G):
                dve.wait_ge(z_ps, g + 1)
                nc.vector.tensor_tensor(u_g[:, g], u_g[:, g], PS[1 + g % 4][:], ALU.mult).then_inc(z_ok, 1)
            dve.wait_ge(c8_ok, 3)
            dve.wait_ge(ld_res, 16)
            for t in range(NT):
                dve.wait_ge(g_ld[t], 16 * K)
                for k in range(K):
                    if k:
                        dve.wait_ge(cmb, (K + 2) * t + k)
                    nc.vector.scalar_tensor_tensor(x_sb[:, t], rows[:, t, k], c8[:, t, k:k + 1], x_sb[:, t],
                                                   ALU.mult, ALU.add).then_inc(cmb, 1)
                dve.wait_ge(o_ps, t + 1)
                dve.wait_ge(cmb, (K + 2) * t + K)
                nc.vector.tensor_tensor(x_sb[:, t], x_sb[:, t], PS[5 + t % 2][:, 0:DM], ALU.add).then_inc(cmb, 2)

        @block.scalar
        def _(act):
            act.wait_ge(zset, 1)
            rows_per = P * 2 * 2 * L // DM
            for i in range(16):
                act.dma_start(slot_x[i * T:(i + 1) * T].rearrange("(p r) d -> p (r d)", p=P), zeros).then_inc(zeroed, 16)
            act.wait_ge(ln, 2 * NT + 1)
            nc.scalar.activation(sd[:], ve[:], ACT.Sqrt).then_inc(sd_ready, 1)
            for h in range(2):
                act.wait_ge(xt_ps, 2 * h + 2)
                nc.scalar.copy(xT[:, 1, h * 512:(h + 1) * 512], PS[2 * h + 1][:]).then_inc(xt_ready, 1)
            act.wait_ge(ld_par, 16)
            nc.scalar.activation(a_pos[:], pars[:, :, ALOG:ALOG + NS], ACT.Exp).then_inc(a_exp, 1)
            act.wait_ge(rt, RT_SUB)
            nc.scalar.activation(prob[:], prob[:], ACT.Exp).then_inc(ac_r, 1)
            act.wait_ge(consts, CONSTS)
            for i in range(G):
                d, b = i // B, i % B
                act.wait_ge(in_ps, i + 1)
                nc.scalar.copy(xpad[:, b, d, DC - 1:], PS[i % 4][:]).then_inc(in_ready, 1)
            for d in range(DT):
                act.wait_ge(conv, DC * (d + 1))
                nc.scalar.activation(u[:, :, d], u[:, :, d], ACT.Silu, bias=pars[:, d, CB:CB + 1]).then_inc(u_ready, 1)
            for b in range(B):
                act.wait_ge(bc_ps, b + 1)
                nc.scalar.copy(bcs[0:2 * NS, b], PS[2 + b][0:2 * NS, :]).then_inc(bc_row, 1)
            for b in range(B):
                act.wait_ge(dr_ps, b + 1)
                nc.scalar.copy(dtr[:, b], PS[b][:]).then_inc(dr_ready, 1)
            act.wait_ge(small, 5)
            for c in range(G // 2):
                for g in (2 * c, 2 * c + 1):
                    act.wait_ge(dt_ps, g + 1)
                    nc.scalar.activation(sp_s[:, g], PS[4 + g % 4][:], ACT.Abs, bias=dtb2[:, g % DT]).then_inc(dt_abs, 1)
                two = slice(2 * c, 2 * c + 2)
                act.wait_ge(dt_abs, 2 * c + 2)
                nc.scalar.activation(sp_s[:, two], sp_s[:, two], ACT.Exp, scale=-1.0).then_inc(sp_a, 1)
                act.wait_ge(sp_a, 4 * c + 1)
                nc.scalar.activation(sp_w[:, two], sp_s[:, two], ACT.Copy, bias=2.0).then_inc(sp_a, 1)
                act.wait_ge(sp_v, 8 * c + 2)
                nc.scalar.activation(sp_w[:, two], sp_s[:, two], ACT.Square).then_inc(sp_a, 1)
                act.wait_ge(sp_a, 4 * c + 3)
                nc.scalar.activation(sp_p, sp_w[:, two], ACT.Copy, bias=ATANH[3], scale=ATANH[4]).then_inc(sp_a, 1)
            act.wait_ge(sp_v, 8 * G // 2)
            act.sem_inc(xc_ok, C)
            act.sem_inc(yc_ok, C)

            def group(g):
                with act.Fori(0, NS // 4) as q:
                    for j4 in range(4):
                        j, i = j4 % 2, j4 // 2
                        n = q * 4 + j4
                        s = g * NS + n
                        act.wait_ge(scan_ok, s + C - 1)
                        act.sem_inc(tick, 1)
                        nc.scalar.activation(DA[j][:], dt_sb[:, bass.ds(g, 1)].rearrange("p a l -> p (a l)"), ACT.Exp,
                                             scale=a_neg[:, bass.ds(g, 1), bass.ds(n, 1)].rearrange("p a l -> p (a l)")).then_inc(dA_ok, 1)
                        act.wait_ge(t_ok, s + 1)
                        act.wait_ge(gu_ok, s + C - 1)
                        nc.scalar.copy(xTs[:, j], XT[j]).then_inc(xc_ok, 1)
                        act.wait_ge(ye_ok, s + 2)
                        if j4 % 2 == 0:
                            act.wait_ge(y_st[i], (g * (NS // 4) + q) * 16 + 16)
                        nc.scalar.copy(ysb[:, i, j], YT[1 - j]).then_inc(yc_ok, 1)
                        act.wait_ge(gu_ok, s + C + 1)
                        act.wait_ge(hh_ok, s + C - 1)
                        nc.scalar.activation(th[:, j], GU[j][:, 0:INTER], ACT.Tanh, scale=0.5).then_inc(th_ok, 1)

            with act.Fori(0, G) as g:
                group(g)

        @block.tensor
        def _(pe):
            pe.wait_ge(consts, CONSTS)
            for h in range(2):
                pe.wait_ge(ln, 2 * NT + 2 + (h + 1) * NT // 2)
                for k in range(KD):
                    for t in range(NT // 2):
                        mm = nc.tensor.transpose(PS[2 * h + k][:, t * P:(t + 1) * P],
                                                 x_sb[:, h * NT // 2 + t, k * P:(k + 1) * P], ident[:])
                    mm.then_inc(xt_ps, 1)
            pe.wait_ge(xt_ready, 4)
            pe.wait_ge(ld_gate, 16)
            for t in range(NT):
                for k in range(KD):
                    mm = nc.tensor.matmul(PS[4][:, t * E:(t + 1) * E], xT[:, k, t * P:(t + 1) * P], wgate[:, k],
                                          start=(k == 0), stop=(k == KD - 1))
            mm.then_inc(pe_r, 1)
            pe.wait_ge(ld_in, 16)
            for i in range(G):
                d, b = i // B, i % B
                if i >= 4:
                    pe.wait_ge(in_ready, i - 3)
                for k in range(KD):
                    mm = nc.tensor.matmul(PS[i % 4][:], win[:, k, d * P:(d + 1) * P], xT[:, k, b * L:(b + 1) * L],
                                          start=(k == 0), stop=(k == KD - 1))
                mm.then_inc(in_ps, 1)
            pe.wait_ge(rt, RT_MASK)
            for t in range(NT):
                mm = nc.tensor.transpose(PS[5 + t // 4][0:E, t % 4 * P:(t % 4 + 1) * P], mask[:, t], ident[:])
            mm.then_inc(pe_r, 1)
            pe.wait_ge(rt, RT_NT)
            nc.tensor.matmul(PS[4][0:E, 0:1], tri[:], n_tile[:], start=True, stop=True).then_inc(pe_r, 1)
            pe.wait_ge(rt, RT_POS)
            for t in range(NT):
                mm = nc.tensor.transpose(PS[7][:, t * E:(t + 1) * E], cum[:, t * P:(t + 1) * P], ident[0:E, 0:E])
            mm.then_inc(pe_r, 1)
            pe.wait_ge(rt, RT_CMP)
            nc.tensor.matmul(PS[4][0:1, P:P + TILES], ones[0:E, 0:1], cmp, start=True, stop=True).then_inc(pe_r, 1)
            pe.wait_ge(u_ready, DT)
            pe.wait_ge(ld_wx, 16)
            pe.wait_ge(in_ready, G)
            for b in range(B):
                for k in range(DT):
                    mm = nc.tensor.matmul(PS[2 + b][0:2 * NS], wx[:, k, R:], u[:, b, k], start=(k == 0), stop=(k == DT - 1))
                mm.then_inc(bc_ps, 1)
            for b in range(B):
                for k in range(DT):
                    mm = nc.tensor.matmul(PS[b][:], wx[:, k, 0:R], u[:, b, k], start=(k == 0), stop=(k == DT - 1))
                mm.then_inc(dr_ps, 1)
            pe.wait_ge(ld_wdt, 16)
            pe.wait_ge(rt, RT_TILE)
            for g in range(G):
                pe.wait_ge(dr_ready, g // DT + 1)
                if g >= 4:
                    pe.wait_ge(dt_max, g - 3)
                nc.tensor.matmul(PS[4 + g % 4][:], wdt[:, g % DT * P:(g % DT + 1) * P], dtr[:, g // DT],
                                 start=True, stop=True).then_inc(dt_ps, 1)
            pe.wait_ge(dt_abs, G)
            pe.wait_ge(dt_max, G)
            pe.sem_inc(gu_ok, C)
            pe.sem_inc(acc_ok, C)
            pe.sem_inc(ye_ok, 1)

            def step(g, q, j4, first):
                j = j4 % 2
                s = g * NS + q * 4 + j4
                if j == 0:
                    pe.wait_ge(xg_ld[j4 // 2], (g * (NS // 4) + q) * 16 + 16)
                pe.wait_ge(xc_ok, s + C)
                for k in range(KD):
                    mm = nc.tensor.transpose(XT[j][:, k * P:(k + 1) * P], xg[:, j4 // 2, j, k * P:(k + 1) * P], ident[:])
                mm.then_inc(t_ok, 1)
                pe.wait_ge(hh_ok, s + C)
                pe.wait_ge(yc_ok, s + C)
                nc.tensor.matmul(YT[1 - j], hh[:, 1 - j], wring[:, (j4 + 3) % 4, 2 * DM:2 * DM + DM],
                                 start=True, stop=True).then_inc(ye_ok, 1)
                pe.wait_ge(w_ld[j4], (g * (NS // 4) + q) * 16 + 16)
                pe.wait_ge(xc_ok, s + C + 1)
                for half in range(2):
                    for k in range(KD):
                        mm = nc.tensor.matmul(GU[j][:, half * P:(half + 1) * P],
                                              wring[:, j4, k * 2 * P + half * P:k * 2 * P + (half + 1) * P],
                                              xTs[:, j, k * P:(k + 1) * P], start=(k == 0), stop=(k == KD - 1))
                mm.then_inc(gu_ok, 1)
                pe.wait_ge(hc_ok, s + C + 1)
                if first:
                    pe.wait_ge(y_out, g + 1)
                nc.tensor.matmul(Y_ACC[:], ident[:], hc[:, j], start=first, stop=True, skip_group_check=True).then_inc(acc_ok, 1)

            with pe.Fori(0, G) as g:
                for j4 in range(4):
                    step(g, 0, j4, j4 == 0)
                with pe.Fori(1, NS // 4) as q:
                    for j4 in range(4):
                        step(g, q, j4, False)
            for g in range(G):
                d, b = g % DT, g // DT
                if g >= 4:
                    pe.wait_ge(z_ok, g - 3)
                for k in range(KD):
                    mm = nc.tensor.matmul(PS[1 + g % 4][:], win[:, k, DI + d * P:DI + (d + 1) * P], xT[:, k, b * L:(b + 1) * L],
                                          start=(k == 0), stop=(k == KD - 1))
                mm.then_inc(z_ps, 1)
            pe.wait_ge(ld_wout, 16)
            for t in range(NT):
                b, c = t // (L // P), t % (L // P)
                pe.wait_ge(z_ok, (b + 1) * DT)
                if t >= 2:
                    pe.wait_ge(cmb, (K + 2) * (t - 1))
                for k in range(DT):
                    mm = nc.tensor.matmul(PS[5 + t % 2][:, 0:DM], u[:, b, k, c * P:(c + 1) * P], wout[:, k],
                                          start=(k == 0), stop=(k == DT - 1))
                mm.then_inc(o_ps, 1)


def kernel(**inputs):
    import numpy as np
    import concourse.bacc as bacc
    from concourse.bass_utils import run_bass_kernel_spmd as run

    a = {k: np.asarray(v) for k, v in inputs.items()}
    x = a["L0_attn_hidden_states"].reshape(T, DM)
    par = np.concatenate([a["L0_attn_conv_w"], a["L0_attn_conv_b"][:, None], a["L0_attn_dt_proj_b"][:, None],
                          a["L0_attn_D"][:, None], a["L0_attn_A_log"]], axis=1)
    w13 = a["L0_ffn_w13"].transpose(0, 2, 1)
    w13 = w13.reshape(E, KD, P, 2 * INTER).transpose(0, 2, 1, 3).reshape(E, P, KD * 2 * INTER)
    w_moe = np.concatenate([w13, a["L0_ffn_w2"].transpose(0, 2, 1)], axis=2)
    arrays = {
        "x": x, "w_in": a["L0_attn_in_proj_w"].T, "par": par, "w_x": a["L0_attn_x_proj_w"].T,
        "w_dt": a["L0_attn_dt_proj_w"].T, "w_out": a["L0_attn_out_proj_w"].T, "w_gate": a["L0_ffn_gate_w"].T,
        "w_moe": w_moe,
    }
    arrays = {k: np.ascontiguousarray(v) for k, v in arrays.items()}
    nc = bacc.Bacc("TRN2", target_bir_lowering=False, num_devices=1)
    args = [nc.dram_tensor(k, v.shape, F32, kind="ExternalInput").ap() for k, v in arrays.items()]
    out = nc.dram_tensor("out", (T, DM), F32, kind="ExternalOutput").ap()
    bc_dram = nc.dram_tensor("bc_dram", (2 * NS, T), F32).ap()
    slot_x = nc.dram_tensor("slot_x", (TILES * P, DM), F32).ap()
    slot_y = nc.dram_tensor("slot_y", (TILES * P, DM), F32).ap()
    program(nc, *args, out, bc_dram, slot_x, slot_y)
    r = run(nc, [arrays], core_ids=[0])
    return r.results[0]["out"].reshape(B, L, DM)
```

```python
from contextlib import ExitStack

import concourse.bass as bass
from concourse import mybir

F32 = mybir.dt.float32
I32 = mybir.dt.int32
U32 = mybir.dt.uint32
ALU = mybir.AluOpType
ACT = mybir.ActivationFunctionType
AX = mybir.AxisListType

P = 128
B, L, DM = 2, 512, 256
DI, NS, DC, R = 512, 16, 4, 128
E, K, INTER = 64, 8, 128
T = B * L
NT = T // P
KD = DM // P
DT = DI // P
G = B * DT
UNITS = G * NS
TILES = T * K // P + E
WCOL = KD * 2 * INTER + DM
EPS = 1e-5
C = 2
V3 = 2
CW, CB, DTB, DSKIP, ALOG, NPAR = 0, DC, DC + 1, DC + 2, DC + 3, DC + 3 + NS

assert UNITS == P and TILES == 128 and NT == G and L == 512 and DM == 2 * P and 2 * INTER == DM


def program(nc, x, w_in, par, w_x, w_dt, w_out, w_gate, w_moe, out, bc_dram, slot_x, slot_y):
    with ExitStack() as ctx:
        def sb(name, shape, dt=F32):
            return ctx.enter_context(nc.sbuf_tensor(name, shape, dt))

        def sem(name):
            return ctx.enter_context(nc.semaphore(name))

        x_sb = sb("x_sb", [P, NT, DM])
        xT = sb("xT", [P, KD, T])
        win = sb("win", [P, KD, 2 * DI])
        xpad = sb("xpad", [P, B, DT, L + DC - 1])
        u = sb("u", [P, B, DT, L])
        dt_sb = sb("dt_sb", [P, G, L])
        dtu = sb("dtu", [P, G, L])
        bc = sb("bc", [P, NS, 2, L])
        wring = sb("wring", [P, 4, WCOL])
        prob = sb("prob", [P, NT, E])
        mask = sb("mask", [P, NT, E])
        key = sb("key", [P, NT, E])
        dbu = sb("dbu", [P, 2, L])
        hc = sb("hc", [P, 2, L])
        wx = sb("wx", [P, DT, R + 2 * NS])
        wdt = sb("wdt", [P, DI])
        wout = sb("wout", [P, DT, DM])
        wgate = sb("wgate", [P, KD, E])
        ident = sb("ident", [P, P])
        ones = sb("ones", [P, P])
        tri = sb("tri", [E, E])
        thr = sb("thr", [E, 8])
        tau = sb("tau", [E, TILES])
        pars = sb("pars", [P, DT, NPAR])
        a_neg = sb("a_neg", [P, G, NS])
        a_pos = sb("a_pos", [P, DT, NS])
        d_col = sb("d_col", [P, G, 1])
        dtb2 = sb("dtb2", [P, DT, 1])
        stats = sb("stats", [P, NT, 6])
        mv = sb("mv", [P, NT, 2])
        ve = sb("ve", [P, NT])
        sd = sb("sd", [P, NT])
        rstd = sb("rstd", [P, NT])
        mx = sb("mx", [P, NT])
        sm = sb("sm", [P, NT])
        rs = sb("rs", [P, NT])
        m8 = sb("m8", [P, NT, K])
        k8 = sb("k8", [P, NT, K])
        c8 = sb("c8", [P, NT, K])
        c8_junk = sb("c8_junk", [P, 2, E])
        slot = sb("slot", [P, NT * K], U32)
        slot_r = sb("slot_r", [P, NT * K], U32)
        n_tile = sb("n_tile", [E, 1])
        n_junk = sb("n_junk", [E, 8])
        base = sb("base", [E, 1])
        upto = sb("upto", [E, 1])
        tile_e = sb("tile_e", [1, TILES], I32)
        xg = sb("xg", [P, 2, 2, DM])
        xTs = sb("xTs", [P, 2, DM])
        th = sb("th", [P, 2, INTER])
        gt = sb("gt", [P, INTER])
        hh = sb("hh", [P, 2, INTER])
        ysb = sb("ysb", [P, 2, 2, DM])
        hp = sb("hp", [P, L])
        PS = [ctx.enter_context(nc.psum_tensor(f"bank{i}", [P, 512], F32)) for i in range(8)]

        zeros = bc[:, 0:2].rearrange("p a b l -> p (a b l)")
        wflat = wring[0:E].rearrange("p a b -> p (a b)")
        cum, cmp = wflat[:, 0:T], wflat[:, T:T + TILES]
        bcs = dbu
        dtr = hc
        xpad_f = xpad[:].rearrange("p b d l -> p (b d l)")[:, 0:G * L].rearrange("p (g l) -> p g l", g=G)
        sp_e = xpad_f
        z_sb = xpad_f
        sp_l = dtu
        sp_d = ysb[:].rearrange("p a b d -> p a (b d)")
        diag = wring[:].rearrange("p a b -> p (a b)")[:, 0:K * P].rearrange("p (k q) -> p k q", k=K)
        u_g = u[:].rearrange("p b d l -> p (b d) l")
        rows = [xT[:].rearrange("p k t -> p (k t)").rearrange("p (k d) -> p k d", k=K),
                win[:].rearrange("p k e -> p (k e)").rearrange("p (k d) -> p k d", k=K),
                dt_sb[:, 0:DT].rearrange("p g l -> p (g l)").rearrange("p (k d) -> p k d", k=K),
                dtu[:, 0:DT].rearrange("p g l -> p (g l)").rearrange("p (k d) -> p k d", k=K)]
        Y_ACC, DA, H, XT, GU, YT = PS[0], [PS[1], PS[2]], PS[3], PS[4], [PS[5], PS[6]], PS[7]
        COMB = [PS[4], PS[5]]
        OUT = [PS[6], PS[7], PS[4], PS[5], PS[6], PS[7]]

        ld_x, ld_x1, ld_gate, ld_in, ld_par, ld_wx, ld_wdt, ld_wout = map(
            sem, "ld_x ld_x1 ld_gate ld_in ld_par ld_wx ld_wdt ld_wout".split())
        consts, zset = sem("consts"), sem("zset")
        zeroed = sem("zeroed")
        ln, sd_ready = sem("ln"), sem("sd_ready")
        xt_ps, xt_ready = sem("xt_ps"), sem("xt_ready")
        pe_r, rt, ac_r = sem("pe_r"), sem("rt"), sem("ac_r")
        in_ps, in_ready, in_tap = sem("in_ps"), sem("in_ready"), sem("in_tap")
        conv = [sem(f"conv{d}") for d in range(DT)]
        u_ready = sem("u_ready")
        bc_ps, bc_row, bc_st, bc_ld = map(sem, "bc_ps bc_row bc_st bc_ld".split())
        bc_ld1 = [sem(f"bc_ld1_{q}") for q in range(NS // 4)]
        dr_ps, dr_ready = sem("dr_ps"), sem("dr_ready")
        dt_ps, dt_abs, dt_max = sem("dt_ps"), sem("dt_abs"), sem("dt_max")
        sp_x, sp_ln, sp_v, a_exp, small = map(sem, "sp_x sp_ln sp_v a_exp small".split())
        scat, ld_res = sem("scat"), sem("ld_res")
        dA_ok, dbu_ok, dbv_ok, scan_ok, hc_ok, hp_ok, acc_ok, y_out, yz_ok = map(
            sem, "dA_ok dbu_ok dbv_ok scan_ok hc_ok hp_ok acc_ok y_out yz_ok".split())
        xg_ld = [sem("xg_ld0"), sem("xg_ld1")]
        w_ld = [sem(f"w_ld{i}") for i in range(4)]
        y_st = [sem("y_st0"), sem("y_st1")]
        t_ok, xc_ok, gu_ok, th_ok, gt_ok, hh_ok, ye_ok, yc_ok = map(
            sem, "t_ok xc_ok gu_ok th_ok gt_ok hh_ok ye_ok yc_ok".split())
        tick = sem("tick")
        g_ld = [sem(f"g_ld{i}") for i in range(4)]
        z_ps, z_ok, c8_ok = map(sem, "z_ps z_ok c8_ok".split())
        dg_ok, cb_ok, cb_out, o_ps, fin, o_st = map(sem, "dg_ok cb_ok cb_out o_ps fin o_st".split())

        x_t = x.rearrange("(t p) d -> p t d", p=P)
        out_t = out.rearrange("(t p) d -> p t d", p=P)
        slot_x_t = slot_x.rearrange("(i j p) d -> i p j d", j=2, p=P)
        slot_y_t = slot_y[0:TILES * P].rearrange("(i j p) d -> i p j d", j=2, p=P)
        bc_v = bc_dram.rearrange("(c n) (b l) -> b c n l", c=2, b=B)
        CONSTS = 9
        RT_SUB, RT_PROB, RT_MAX, RT_REP, RT_MASK = 2, 5, 5 + NT, 5 + 2 * NT, 6 + 2 * NT
        RT_CUM0, RT_CUM, RT_NT, RT_BASE, RT_UPTO, RT_POS, RT_CMP, RT_KEY = range(RT_MASK + 1, RT_MASK + 9)
        RT_K8 = RT_KEY + NT
        RT_SLOT, RT_SLOT1, RT_TILE = RT_K8 + 1, RT_K8 + 2, RT_K8 + 3
        SP_STEPS = 5
        G1, G2, G3 = 1, 1 + DT, G - 1
        QG = NS // 2
        ZERO_DMAS = 16
        PARTS = [(0, 2), (2, 4), (4, 5), (5, 6), (6, 7), (7, 8)]
        block = ctx.enter_context(nc.Block())

        def at(t, i):
            return t[:, bass.ds(i, 1)].rearrange("p a l -> p (a l)")

        @block.sync
        def _(sp):
            sp.dma_start(x_sb[:, 0:NT // 2], x_t[:, 0:NT // 2]).then_inc(ld_x, 16)
            sp.dma_start(x_sb[:, NT // 2:NT], x_t[:, NT // 2:NT]).then_inc(ld_x1, 16)
            sp.dma_start(wgate[:], w_gate.rearrange("(k p) e -> p k e", p=P)).then_inc(ld_gate, 16)
            sp.dma_start(win[:], w_in.rearrange("(k p) e -> p k e", p=P)).then_inc(ld_in, 16)
            sp.dma_start(pars[:], par.rearrange("(t p) n -> p t n", p=P)).then_inc(ld_par, 16)
            sp.wait_ge(zset, 1)
            n = TILES * P // ZERO_DMAS
            for i in range(ZERO_DMAS):
                sp.dma_start(slot_x[i * n:(i + 1) * n].rearrange("(p r) d -> p (r d)", p=P), zeros).then_inc(zeroed, 16)
                if i == 0:
                    sp.dma_start(wx[:], w_x.rearrange("(t p) n -> p t n", p=P)).then_inc(ld_wx, 16)
                    sp.dma_start(wdt[:], w_dt).then_inc(ld_wdt, 16)
                    sp.dma_start(wout[:], w_out.rearrange("(t p) n -> p t n", p=P)).then_inc(ld_wout, 16)
            sp.wait_ge(bc_row, B)
            sp.dma_start(bc_dram, bcs[0:2 * NS].rearrange("p b l -> p (b l)")).then_inc(bc_st, 16)
            sp.wait_ge(bc_st, 16)
            sp.wait_ge(zeroed, 16 * ZERO_DMAS)
            sp.wait_ge(rt, RT_CUM)

            def spread(b, q, done):
                for c in range(2):
                    sp.dma_start(bc[:, 4 * q:4 * q + 4, c], bc_v[b, c, 4 * q:4 * q + 4].partition_broadcast(P)).then_inc(done, 16)

            for q in range(NS // 4):
                spread(0, q, bc_ld)
            sp.wait_ge(rt, RT_TILE)
            for j in range(2):
                sp.sem_inc(y_st[j], 16)
            sp.sem_inc(w_ld[3], 16)

            def load_w(v, j, wait=True):
                e = sp.value_load(tile_e[0:1, bass.ds(v, 1)], min_val=0, max_val=E - 1)
                if wait:
                    sp.wait_ge(ye_ok, v - 1 + C)
                sp.dma_start(wring[:, j], w_moe[bass.ds(e, 1)].rearrange("a p n -> p (a n)")).then_inc(w_ld[j], 16)

            def load_x(i, j):
                sp.dma_start(xg[:, j], slot_x_t[bass.ds(i, 1)].rearrange("a p j d -> p (a j) d")).then_inc(xg_ld[j], 16)

            def store_y(i, j):
                sp.dma_start(slot_y_t[bass.ds(i, 1)].rearrange("a p j d -> p (a j) d"), ysb[:, j]).then_inc(y_st[j], 16)

            load_w(0, 0, False)
            load_w(1, 1, False)
            sp.wait_ge(scat, 16 * NT * K)
            load_x(0, 0)
            load_x(1, 1)
            sp.dma_start(x_sb[:], x_t).then_inc(ld_res, 16)

            def quad(Q, last=False):
                load_w(4 * Q + 2, 2)
                if not last:
                    sp.wait_ge(t_ok, 4 * Q + 2)
                    load_x(2 * Q + 2, 0)
                load_w(4 * Q + 3, 3)
                sp.wait_ge(yc_ok, 4 * Q + 2 + C)
                store_y(2 * Q, 0)
                if not last:
                    load_w(4 * Q + 4, 0)
                    sp.wait_ge(t_ok, 4 * Q + 4)
                    load_x(2 * Q + 3, 1)
                    load_w(4 * Q + 5, 1)
                sp.wait_ge(yc_ok, 4 * Q + 4 + C)
                store_y(2 * Q + 1, 1)

            with sp.Fori(0, (DT - 1 - G1) * QG) as Q:
                quad(Q)
            for q in range(NS // 4):
                with sp.Fori((DT - 1 - G1) * QG + 2 * q, (DT - 1 - G1) * QG + 2 * q + 2) as Q:
                    quad(Q)
                done = (DT - 1) * NS + 4 * q + 4
                sp.wait_ge(hc_ok, done + C)
                sp.wait_ge(dbu_ok, done - G1 * NS)
                spread(1, q, bc_ld1[q])
            with sp.Fori((DT - G1) * QG, TILES // 4 - 1) as Q:
                quad(Q)
            quad(TILES // 4 - 1, last=True)
            sp.wait_ge(yc_ok, TILES + 1 + C)
            sp.dma_start(slot_y[TILES * P:(TILES + 1) * P], ysb[:, 0, 0]).then_inc(y_st[0], 16)
            for i, (t0, t1) in enumerate(PARTS):
                sp.wait_ge(fin, i + 1)
                sp.dma_start(out_t[:, t0:t1], x_sb[:, t0:t1]).then_inc(o_st, 16)
            sp.wait_ge(o_st, 16 * len(PARTS))

        @block.gpsimd
        def _(pool):
            nc.gpsimd.memset(zeros, 0.0).then_inc(zset, 1)
            nc.gpsimd.memset(ones[:], 1.0).then_inc(consts, 1)
            nc.gpsimd.memset(xpad[:, :, :, 0:DC - 1], 0.0).then_inc(consts, 1)
            nc.gpsimd.iota(thr[:], [[P, 8]], base=0, channel_multiplier=0,
                           allow_small_or_imprecise_dtypes=True).then_inc(consts, 1)
            nc.gpsimd.iota(tau[:], [[1, TILES]], base=0, channel_multiplier=0,
                           allow_small_or_imprecise_dtypes=True).then_inc(consts, 1)
            nc.gpsimd.memset(hh[:], 0.0).then_inc(consts, 1)
            nc.gpsimd.memset(xTs[:, 1], 0.0).then_inc(consts, 1)
            nc.gpsimd.memset(wring[:, 2:4], 0.0).then_inc(consts, 1)
            pool.wait_ge(consts, 7)
            nc.gpsimd.affine_select(out=ident[:], in_=ones[:], compare_op=ALU.is_equal, fill=0.0, base=0,
                                    pattern=[[-1, P]], channel_multiplier=1).then_inc(consts, 1)
            nc.gpsimd.affine_select(out=tri[:], in_=ones[0:E, 0:E], compare_op=ALU.is_gt, fill=0.0, base=0,
                                    pattern=[[1, E]], channel_multiplier=-1).then_inc(consts, 1)
            pool.wait_ge(consts, CONSTS)
            pool.wait_ge(rt, RT_SLOT)
            pool.wait_ge(zeroed, 16 * ZERO_DMAS)
            for t in range(NT):
                for k in range(K):
                    pool.indirect_dma_start(
                        slot_x, bass.IndirectOffsetOnAxis(ap=slot[:, t * K + k:t * K + k + 1], axis=0),
                        x_sb[:, t, :], None).then_inc(scat, 16)

            def spread_u(g, n, j):
                pool.wait_ge(scan_ok, g * NS + n + C - 1)
                pool.sem_inc(tick, 1)
                nc.gpsimd.tensor_tensor(dbu[:, j], at(dtu, g), bc[:, bass.ds(n, 1), 0].rearrange(
                    "p a l -> p (a l)"), ALU.mult).then_inc(dbu_ok, 1)

            def add_pair(r):
                pool.wait_ge(hc_ok, G1 * NS + 2 * r + 2 + C)
                pool.wait_ge(acc_ok, G1 * NS + 2 * r + C)
                nc.gpsimd.tensor_tensor(hp[:], hc[:, 0], hc[:, 1], ALU.add).then_inc(hp_ok, 1)

            def pair(g, q):
                spread_u(g, 2 * q, 0)
                add_pair((g - G1) * QG + q - 1)
                spread_u(g, 2 * q + 1, 1)

            for j in range(2):
                spread_u(G1, j, j)
            with pool.Fori(1, QG) as q:
                pair(G1, q)
            with pool.Fori(G1 + 1, DT) as g:
                with pool.Fori(0, QG) as q:
                    pair(g, q)
            for h in range(NS // 4):
                pool.wait_ge(bc_ld1[h], 32)
                with pool.Fori(2 * h, 2 * h + 2) as q:
                    pair(DT, q)
            add_pair((G2 - G1) * QG - 1)
            pool.wait_ge(y_st[0], 16 * (TILES // 4 + 1) + 16)
            pool.wait_ge(y_st[1], 16 * (TILES // 4) + 16)
            pool.wait_ge(z_ps, G)
            pool.wait_ge(dA_ok, DT * NS)
            pool.wait_ge(dbu_ok, (DT - 1) * NS)
            pool.wait_ge(dbv_ok, NS)
            for t in range(NT):
                if t >= 4:
                    pool.wait_ge(cb_ok, K * (t - 2))
                for k in range(K):
                    pool.indirect_dma_start(
                        rows[t % 4][:, k, :], None, slot_y,
                        bass.IndirectOffsetOnAxis(ap=slot_r[:, t * K + k:t * K + k + 1], axis=0)).then_inc(g_ld[t % 4], 16)
            for n in range(NS // 2, NS):
                if n % 3 != V3:
                    spread_u(G3, n, n % 2)

        @block.vector
        def _(dve):
            def conv_block(d):
                dve.wait_ge(in_ready, 2 * d + 2)
                dve.wait_ge(in_tap, 2 * d + 2)
                for j in range(DC - 1):
                    if j:
                        dve.wait_ge(conv[d], j)
                    nc.vector.scalar_tensor_tensor(u[:, :, d], xpad[:, :, d, j:j + L], pars[:, d, CW + j:CW + j + 1],
                                                   u[:, :, d], ALU.mult, ALU.add).then_inc(conv[d], 1)

            for t in range(NT):
                if t % (NT // 2) == 0:
                    dve.wait_ge([ld_x, ld_x1][t // (NT // 2)], 16)
                nc.vector.bn_stats(stats[:, t], x_sb[:, t]).then_inc(ln, 1)
            dve.wait_ge(ln, NT)
            for t in range(NT):
                nc.vector.bn_aggr(mv[:, t], stats[:, t]).then_inc(ln, 1)
            dve.wait_ge(ln, 2 * NT)
            nc.vector.tensor_scalar(ve[:], mv[:, :, 1], EPS, None, ALU.add).then_inc(ln, 1)
            dve.wait_ge(sd_ready, 1)
            nc.vector.reciprocal(rstd[:], sd[:]).then_inc(ln, 1)
            dve.wait_ge(ln, 2 * NT + 2)
            for t in range(NT):
                nc.vector.tensor_scalar(x_sb[:, t], x_sb[:, t], mv[:, t, 0:1], rstd[:, t:t + 1],
                                        ALU.subtract, ALU.mult).then_inc(ln, 1)
            for h in range(2):
                dve.wait_ge(xt_ps, 2 * h + 1)
                nc.vector.tensor_copy(xT[:, 0, h * 512:(h + 1) * 512], PS[2 * h][:]).then_inc(xt_ready, 1)
            logit = PS[4][:].rearrange("p (t e) -> p t e", t=NT)
            dve.wait_ge(pe_r, 1)
            nc.vector.tensor_reduce(mx[:], logit, AX.X, ALU.max).then_inc(rt, 1)
            dve.wait_ge(rt, 1)
            nc.vector.tensor_tensor(prob[:], logit, mx[:].unsqueeze(2).broadcast_to([P, NT, E]), ALU.subtract).then_inc(rt, 1)
            dve.wait_ge(ac_r, 1)
            nc.vector.tensor_reduce(sm[:], prob[:], AX.X, ALU.add).then_inc(rt, 1)
            dve.wait_ge(rt, 3)
            nc.vector.reciprocal(rs[:], sm[:]).then_inc(rt, 1)
            dve.wait_ge(rt, 4)
            nc.vector.tensor_tensor(prob[:], prob[:], rs[:].unsqueeze(2).broadcast_to([P, NT, E]), ALU.mult).then_inc(rt, 1)
            dve.wait_ge(rt, RT_PROB)
            for t in range(NT):
                nc.vector.max(m8[:, t], prob[:, t]).then_inc(rt, 1)
            dve.wait_ge(rt, RT_MAX)
            for t in range(NT):
                nc.vector.match_replace(mask[:, t], m8[:, t], prob[:, t], -1.0).then_inc(rt, 1)
            dve.wait_ge(rt, RT_REP)
            nc.vector.tensor_scalar(mask[:], mask[:], 0.0, None, ALU.is_lt).then_inc(rt, 1)
            dve.wait_ge(ld_par, 16)
            dve.wait_ge(consts, CONSTS)
            conv_block(0)
            dve.wait_ge(pe_r, 2)
            dve.wait_ge(zset, 1)
            zrow = zeros[0:E, 0:512]
            nc.vector.tensor_tensor_scan(cum[:, 0:512], zrow, PS[5][0:E, :], 0.0, ALU.add, ALU.add).then_inc(rt, 1)
            dve.wait_ge(rt, RT_CUM0)
            nc.vector.tensor_tensor_scan(cum[:, 512:1024], zrow, PS[6][0:E, :], cum[:, 511:512], ALU.add, ALU.add).then_inc(rt, 1)
            dve.wait_ge(rt, RT_CUM)
            nc.vector.tensor_scalar(n_junk[:], thr[:], cum[:, T - 1:T], None, ALU.is_lt, ALU.add,
                                    accum_out=n_tile[:]).then_inc(rt, 1)
            dve.wait_ge(pe_r, 3)
            nc.vector.tensor_scalar(base[:], PS[4][0:E, 0:1], float(P), None, ALU.mult).then_inc(rt, 1)
            dve.wait_ge(rt, RT_NT)
            nc.vector.tensor_tensor(upto[:], PS[4][0:E, 0:1], n_tile[:], ALU.add).then_inc(rt, 1)
            dve.wait_ge(rt, RT_BASE)
            nc.vector.tensor_scalar(cum, cum, base[:], None, ALU.add).then_inc(rt, 1)
            dve.wait_ge(rt, RT_UPTO)
            nc.vector.tensor_scalar(cmp, tau[:], upto[:], None, ALU.is_ge).then_inc(rt, 1)
            dve.wait_ge(pe_r, 4)
            nc.vector.tensor_tensor(key[:].rearrange("p t e -> p (t e)"), mask[:].rearrange("p t e -> p (t e)"),
                                    PS[7][:], ALU.mult).then_inc(rt, 1)
            dve.wait_ge(rt, RT_KEY)
            for t in range(NT):
                nc.vector.max(k8[:, t], key[:, t]).then_inc(rt, 1)
            dve.wait_ge(rt, RT_K8)
            k8f = k8[:].rearrange("p t k -> p (t k)")
            nc.vector.tensor_scalar(slot[:], k8f, -1.0, None, ALU.add).then_inc(rt, 1)
            nc.vector.tensor_scalar(slot_r[:], k8f, float(2 * P - 1), None, ALU.add).then_inc(rt, 1)
            dve.wait_ge(pe_r, 5)
            nc.vector.tensor_scalar(tile_e[:], PS[4][0:1, P:P + TILES], float(E - 1), None, ALU.min).then_inc(rt, 1)
            for d in range(1, DT):
                conv_block(d)
            dve.wait_ge(a_exp, 1)
            for b in range(B):
                nc.vector.tensor_scalar(a_neg[:, b * DT:(b + 1) * DT], a_pos[:], -1.0, None, ALU.mult).then_inc(small, 1)
                nc.vector.tensor_copy(d_col[:, b * DT:(b + 1) * DT], pars[:, :, DSKIP:DSKIP + 1]).then_inc(small, 1)
            nc.vector.tensor_scalar(dtb2[:], pars[:, :, DTB:DTB + 1], 2.0, None, ALU.mult).then_inc(small, 1)
            dve.wait_ge(small, 5)

            def over_zero(g):
                dve.wait_ge(dt_abs, g + 1)
                nc.vector.tensor_scalar(dt_sb[:, g], PS[4 + g % 4][:], dtb2[:, g % DT], 0.0, ALU.add, ALU.max).then_inc(dt_max, 1)

            def softplus(g):
                d, n = sp_d[:, g % 2], SP_STEPS * g
                dve.wait_ge(sp_x, g + 1)
                nc.vector.tensor_scalar(d, sp_e[:, g], 1.0, -1.0, ALU.add, ALU.add).then_inc(sp_v, 1)
                dve.wait_ge(sp_v, n + 1)
                nc.vector.tensor_tensor(d, sp_e[:, g], d, ALU.subtract).then_inc(sp_v, 1)
                dve.wait_ge(sp_v, n + 2)
                dve.wait_ge(sp_ln, g + 1)
                nc.vector.tensor_tensor(d, sp_l[:, g], d, ALU.add).then_inc(sp_v, 1)
                dve.wait_ge(sp_v, n + 3)
                dve.wait_ge(dt_max, g + 1)
                nc.vector.tensor_tensor(dt_sb[:, g], dt_sb[:, g], d, ALU.add).then_inc(sp_v, 1)
                dve.wait_ge(sp_v, n + 4)
                nc.vector.tensor_tensor(dtu[:, g], dt_sb[:, g], u_g[:, g], ALU.mult).then_inc(sp_v, 1)

            for g in range(G):
                over_zero(g)
            for g in range(G):
                softplus(g)
            dve.wait_ge(sp_v, SP_STEPS * G)
            for s_ in (scan_ok, hc_ok, hh_ok):
                dve.sem_inc(s_, C)
            dve.sem_inc(y_out, 1)

            def spread_u(g, n, j, count):
                s = g * NS + n
                dve.wait_ge(scan_ok, s + C - 1)
                nc.vector.tensor_tensor(dbu[:, j], at(dtu, g), bc[:, bass.ds(n, 1), 0].rearrange("p a l -> p (a l)"),
                                        ALU.mult).then_inc(dbv_ok, 1)
                dve.wait_ge(dbv_ok, count)

            def scan(g, n, j):
                s = g * NS + n
                dve.wait_ge(dA_ok, s + 1)
                dve.wait_ge(hc_ok, s + C)
                nc.vector.tensor_tensor_scan(H[:], DA[j][:], dbu[:, j], 0.0, ALU.mult, ALU.add).then_inc(scan_ok, 1)

            def times_c(g, n, j, alone=True):
                s = g * NS + n
                if alone:
                    dve.wait_ge(acc_ok, s + C - 1)
                dve.wait_ge(scan_ok, s + C + 1)
                nc.vector.tensor_tensor(hc[:, j], H[:], bc[:, bass.ds(n, 1), 1].rearrange("p a l -> p (a l)"),
                                        ALU.mult).then_inc(hc_ok, 1)

            def finish_group(g):
                dve.wait_ge(acc_ok, (g + 1) * NS + C)
                nc.vector.scalar_tensor_tensor(at(u_g, g), at(u_g, g), at(d_col, g), Y_ACC[:], ALU.mult, ALU.add).then_inc(y_out, 1)
                dve.wait_ge(y_out, g + 2)
                nc.vector.tensor_tensor(at(u_g, g), at(u_g, g), at(z_sb, g), ALU.mult).then_inc(yz_ok, 1)

            def hidden(v, j):
                dve.wait_ge(th_ok, v + 1)
                dve.wait_ge(hh_ok, v + C)
                nc.vector.scalar_tensor_tensor(gt[:], th[:, 1 - j], 1.0, GU[1 - j][:, 0:INTER], ALU.add, ALU.mult).then_inc(gt_ok, 1)
                dve.wait_ge(ye_ok, v + C)
                dve.wait_ge(gt_ok, v + 1)
                nc.vector.scalar_tensor_tensor(hh[:, 1 - j], gt[:], 0.5, GU[1 - j][:, INTER:2 * INTER],
                                               ALU.mult, ALU.mult).then_inc(hh_ok, 1)

            def pair0(g, q, count):
                for j in range(2):
                    spread_u(g, 2 * q + j, j, count + 2 * q + j + 1)
                    scan(g, 2 * q + j, j)
                    times_c(g, 2 * q + j, j)

            dve.wait_ge(bc_ld, 32 * (NS // 4))
            with dve.Fori(0, NS // 2) as q:
                pair0(0, q, 0)

            def pair1(g, q):
                for j in range(2):
                    n, r = 2 * q + j, (g - G1) * QG + q
                    v = 4 * r + 2 * j
                    dve.wait_ge(dbu_ok, (g - G1) * NS + n + 1)
                    scan(g, n, j)
                    hidden(v, 0)
                    if j == 0:
                        dve.wait_ge(hp_ok, r + 1)
                    times_c(g, n, j, False)
                    hidden(v + 1, 1)
                    k = (g - G1) * 2 + j
                    nc.vector.scalar_tensor_tensor(
                        c8_junk[:, j], at(key, q), k8[:, bass.ds(q, 1), bass.ds(k, 1)].rearrange("p a b -> p (a b)"),
                        at(prob, q), ALU.is_equal, ALU.mult,
                        accum_out=c8[:, bass.ds(q, 1), bass.ds(k, 1)].rearrange("p a b -> p (a b)")).then_inc(c8_ok, 1)

            dve.wait_ge(z_ok, G)
            dve.wait_ge(acc_ok, G1 * NS + C)
            dve.sem_inc(hp_ok, 1)
            with dve.Fori(G1, G2) as g:
                pair1(g, 0)
                finish_group(g - 1)
                with dve.Fori(1, QG) as q:
                    pair1(g, q)
            dve.wait_ge(hp_ok, (G2 - G1) * QG + 1)
            def half(g, h, count):
                if h == 0:
                    pair0(g, 0, count)
                    finish_group(g - 1)
                with dve.Fori(h * QG // 2 + (h == 0), (h + 1) * QG // 2) as q:
                    pair0(g, q, count)

            half(G2, 0, NS)
            with dve.Fori(0, 2) as h:
                half(G2 + h, 1, NS + h * NS)
                half(G2 + h + 1, 0, 2 * NS + h * NS)

            def add_out(i):
                t0, t1 = PARTS[i]
                dve.wait_ge(cb_out, NT + 2)
                dve.wait_ge(o_ps, i + 1)
                xo = x_sb[:, t0:t1].rearrange("p t d -> p (t d)")
                nc.vector.tensor_tensor(xo, xo, OUT[i][:, 0:(t1 - t0) * DM], ALU.add).then_inc(fin, 1)

            mine = 0
            for n in range(NS // 2, NS):
                if n % 3 == V3:
                    mine += 1
                    spread_u(G3, n, n % 2, 3 * NS + NS // 2 + mine)
                else:
                    dve.wait_ge(dbu_ok, DT * NS + n + 1 - NS // 2 - mine)
                scan(G3, n, n % 2)
                times_c(G3, n, n % 2)
                if n in (11, 13):
                    add_out((n - 11) // 2)
            finish_group(G3)
            for i in range(2, len(PARTS)):
                add_out(i)

        @block.scalar
        def _(act):
            act.wait_ge(ln, 2 * NT + 1)
            nc.scalar.activation(sd[:], ve[:], ACT.Sqrt).then_inc(sd_ready, 1)
            for h in range(2):
                act.wait_ge(xt_ps, 2 * h + 2)
                nc.scalar.copy(xT[:, 1, h * 512:(h + 1) * 512], PS[2 * h + 1][:]).then_inc(xt_ready, 1)
            act.wait_ge(ld_par, 16)
            nc.scalar.activation(a_pos[:], pars[:, :, ALOG:ALOG + NS], ACT.Exp).then_inc(a_exp, 1)
            act.wait_ge(rt, RT_SUB)
            nc.scalar.activation(prob[:], prob[:], ACT.Exp).then_inc(ac_r, 1)
            act.wait_ge(consts, CONSTS)
            for i in range(G):
                d, b = i // B, i % B
                act.wait_ge(in_ps, i + 1)
                nc.scalar.copy(xpad[:, b, d, DC - 1:], PS[i % 4][:]).then_inc(in_ready, 1)
                nc.scalar.activation(u[:, b, d], PS[i % 4][:], ACT.Copy, scale=pars[:, d, CW + DC - 1:CW + DC]).then_inc(in_tap, 1)
            for d in range(DT):
                act.wait_ge(conv[d], DC - 1)
                nc.scalar.activation(u[:, :, d], u[:, :, d], ACT.Silu, bias=pars[:, d, CB:CB + 1]).then_inc(u_ready, 1)
            for b in range(B):
                act.wait_ge(bc_ps, b + 1)
                nc.scalar.copy(bcs[0:2 * NS, b], PS[2 + b][0:2 * NS, :]).then_inc(bc_row, 1)
            for b in range(B):
                act.wait_ge(dr_ps, b + 1)
                nc.scalar.copy(dtr[:, b], PS[b][:]).then_inc(dr_ready, 1)
            act.wait_ge(small, 5)
            for g in range(G):
                act.wait_ge(dt_ps, g + 1)
                nc.scalar.activation(sp_e[:, g], PS[4 + g % 4][:], ACT.Abs, bias=dtb2[:, g % DT]).then_inc(dt_abs, 1)
                act.wait_ge(dt_abs, g + 1)
                nc.scalar.activation(sp_e[:, g], sp_e[:, g], ACT.Exp, scale=-1.0).then_inc(sp_x, 1)
            for g in range(G):
                act.wait_ge(sp_x, g + 1)
                nc.scalar.activation(sp_l[:, g], sp_e[:, g], ACT.Ln, bias=1.0).then_inc(sp_ln, 1)
            act.wait_ge(sp_v, SP_STEPS * G)
            for s_ in (xc_ok, yc_ok):
                act.sem_inc(s_, C)

            def decay(g, n, j):
                act.wait_ge(scan_ok, g * NS + n + C - 1)
                act.sem_inc(tick, 1)
                nc.scalar.activation(DA[j][:], at(dt_sb, g), ACT.Exp, scale=a_neg[:, bass.ds(g, 1), bass.ds(n, 1)].rearrange(
                    "p a l -> p (a l)")).then_inc(dA_ok, 1)

            with act.Fori(0, B) as b:
                for d in range(DT):
                    for j in range(2):
                        decay(0, b * NS // B + 2 * d + j, j)
                    act.wait_ge(z_ps, b * DT + d + 1)
                    nc.scalar.copy(at(z_sb, b * DT + d), PS[4 + d][:]).then_inc(z_ok, 1)

            def tile_slot(v, Q, j4):
                j, i = j4 % 2, j4 // 2
                act.wait_ge(t_ok, v + 1)
                act.wait_ge(gu_ok, v + C)
                nc.scalar.copy(xTs[:, j], XT[:, 0:DM]).then_inc(xc_ok, 1)
                act.wait_ge(gu_ok, v + C + 1)
                act.wait_ge(hh_ok, v + C - 1)
                nc.scalar.activation(th[:, 1 - j], GU[1 - j][:, 0:INTER], ACT.Tanh, scale=0.5).then_inc(th_ok, 1)
                act.wait_ge(ye_ok, v + C + 1)
                if j == 0:
                    act.wait_ge(y_st[i], Q * 16 + 16)
                nc.scalar.copy(ysb[:, i, j], YT[:, 0:DM]).then_inc(yc_ok, 1)

            with act.Fori(G1, G2) as g:
                with act.Fori(0, QG) as q:
                    for j4 in range(4):
                        Q = (g - G1) * QG + q
                        if j4 % 2 == 0:
                            decay(g, 2 * q + j4 // 2, j4 // 2)
                        tile_slot(Q * 4 + j4, Q, j4)
            act.wait_ge(ye_ok, TILES + C + 1)
            act.wait_ge(y_st[0], (TILES // 4) * 16 + 16)
            nc.scalar.copy(ysb[:, 0, 0], YT[:, 0:DM]).then_inc(yc_ok, 1)
            act.wait_ge(c8_ok, NT * K)
            with act.Fori(0, NS // 4) as q:
                for j in range(2):
                    decay(G2, 2 * q + j, j)

            def summed(t, c):
                act.wait_ge(cb_ok, t * K + K + K)
                act.sem_inc(tick, 1)
                nc.scalar.copy(at(x_sb, t), COMB[c % 2][:, 0:DM]).then_inc(cb_out, 1)

            with act.Fori(0, 2) as h:
                for c in range(4):
                    g, q, t = G2 + h + c // 2, (c + 2) % 4, 4 * h + c
                    for i in range(4):
                        decay(g, 4 * q + i, i % 2)
                        if i == 1 and c > 0:
                            summed(t - 1, c - 1)
                        for k in (2 * i, 2 * i + 1):
                            act.wait_ge(cb_ok, t * K + k + 1)
                            act.sem_inc(tick, 1)
                            nc.scalar.activation(diag[:, k], ident[:], ACT.Copy, scale=c8[:, bass.ds(t, 1), k:k + 1].rearrange(
                                "p a b -> p (a b)")).then_inc(dg_ok, 1)
                summed(4 * h + 3, 3)
            with act.Fori(NS // 4, NS // 2) as q:
                for j in range(2):
                    decay(G3, 2 * q + j, j)

        @block.tensor
        def _(pe):
            pe.wait_ge(consts, CONSTS)
            for h in range(2):
                pe.wait_ge(ln, 2 * NT + 2 + (h + 1) * NT // 2)
                for k in range(KD):
                    for t in range(NT // 2):
                        mm = nc.tensor.transpose(PS[2 * h + k][:, t * P:(t + 1) * P],
                                                 x_sb[:, h * NT // 2 + t, k * P:(k + 1) * P], ident[:])
                    mm.then_inc(xt_ps, 1)
            pe.wait_ge(xt_ready, 4)
            pe.wait_ge(ld_gate, 16)
            for t in range(NT):
                for k in range(KD):
                    mm = nc.tensor.matmul(PS[4][:, t * E:(t + 1) * E], xT[:, k, t * P:(t + 1) * P], wgate[:, k],
                                          start=(k == 0), stop=(k == KD - 1))
            mm.then_inc(pe_r, 1)
            pe.wait_ge(ld_in, 16)

            def project_in(i):
                d, b = i // B, i % B
                if i >= 4:
                    pe.wait_ge(in_tap, i - 3)
                for k in range(KD):
                    mm = nc.tensor.matmul(PS[i % 4][:], win[:, k, d * P:(d + 1) * P], xT[:, k, b * L:(b + 1) * L],
                                          start=(k == 0), stop=(k == KD - 1))
                mm.then_inc(in_ps, 1)

            for i in range(4):
                project_in(i)
            pe.wait_ge(rt, RT_MASK)
            for t in range(NT):
                mm = nc.tensor.transpose(PS[5 + t // 4][0:E, t % 4 * P:(t % 4 + 1) * P], mask[:, t], ident[:])
            mm.then_inc(pe_r, 1)
            project_in(4)
            pe.wait_ge(rt, RT_NT)
            nc.tensor.matmul(PS[4][0:E, 0:1], tri[:], n_tile[:], start=True, stop=True).then_inc(pe_r, 1)
            project_in(5)
            pe.wait_ge(rt, RT_POS)
            for t in range(NT):
                mm = nc.tensor.transpose(PS[7][:, t * E:(t + 1) * E], cum[:, t * P:(t + 1) * P], ident[0:E, 0:E])
            mm.then_inc(pe_r, 1)
            pe.wait_ge(rt, RT_CMP)
            nc.tensor.matmul(PS[4][0:1, P:P + TILES], ones[0:E, 0:1], cmp, start=True, stop=True).then_inc(pe_r, 1)
            project_in(6)
            project_in(7)
            pe.wait_ge(ld_wx, 16)
            pe.wait_ge(in_tap, G)
            for k in range(DT):
                pe.wait_ge(u_ready, k + 1)
                for b in range(B):
                    mm = nc.tensor.matmul(PS[2 + b][0:2 * NS], wx[:, k, R:], u[:, b, k], start=(k == 0), stop=(k == DT - 1))
                    if k == DT - 1:
                        mm.then_inc(bc_ps, 1)
                for b in range(B):
                    mm = nc.tensor.matmul(PS[b][:], wx[:, k, 0:R], u[:, b, k], start=(k == 0), stop=(k == DT - 1))
                    if k == DT - 1:
                        mm.then_inc(dr_ps, 1)
            pe.wait_ge(ld_wdt, 16)
            pe.wait_ge(rt, RT_TILE)
            for g in range(G):
                pe.wait_ge(dr_ready, g // DT + 1)
                if g >= 4:
                    pe.wait_ge(dt_max, g - 3)
                nc.tensor.matmul(PS[4 + g % 4][:], wdt[:, g % DT * P:(g % DT + 1) * P], dtr[:, g // DT],
                                 start=True, stop=True).then_inc(dt_ps, 1)
            pe.wait_ge(dt_max, G)
            for s_ in (gu_ok, acc_ok, ye_ok):
                pe.sem_inc(s_, C)
            pe.sem_inc(cb_ok, K)
            pe.sem_inc(cb_out, 2)

            def sum_states(g, n, j, first):
                pe.wait_ge(hc_ok, g * NS + n + C + 1)
                if first:
                    pe.wait_ge(y_out, g + 1)
                nc.tensor.matmul(Y_ACC[:], ident[:], hc[:, j], start=first, stop=True, skip_group_check=True).then_inc(acc_ok, 1)

            for i in range(G):
                d, b = i % DT, i // DT
                if i >= 4:
                    pe.wait_ge(z_ok, i - 3)
                for k in range(KD):
                    mm = nc.tensor.matmul(PS[4 + d][:], win[:, k, DI + d * P:DI + (d + 1) * P], xT[:, k, b * L:(b + 1) * L],
                                          start=(k == 0), stop=(k == KD - 1))
                mm.then_inc(z_ps, 1)
                for j in range(2):
                    sum_states(0, 2 * i + j, j, i + j == 0)
            pe.wait_ge(z_ok, G)

            def tile_slot(v, Q, j4):
                j = j4 % 2
                if j == 0:
                    pe.wait_ge(xg_ld[j4 // 2], Q * 16 + 16)
                pe.wait_ge(xc_ok, v + C)
                for k in range(KD):
                    mm = nc.tensor.transpose(XT[:, k * P:(k + 1) * P], xg[:, j4 // 2, j, k * P:(k + 1) * P], ident[:])
                mm.then_inc(t_ok, 1)
                w = (j4 + 3) % 4
                pe.wait_ge(w_ld[w], Q * 16 + 16)
                pe.wait_ge(hh_ok, v + C - 1)
                for half in range(2):
                    for k in range(KD):
                        mm = nc.tensor.matmul(GU[1 - j][:, half * P:(half + 1) * P],
                                              wring[:, w, k * 2 * P + half * P:k * 2 * P + (half + 1) * P],
                                              xTs[:, 1 - j, k * P:(k + 1) * P], start=(k == 0), stop=(k == KD - 1))
                mm.then_inc(gu_ok, 1)
                down(v, j, (j4 + 2) % 4)

            def down(v, j, w):
                pe.wait_ge(hh_ok, v + C)
                pe.wait_ge(yc_ok, v + C)
                nc.tensor.matmul(YT[:, 0:DM], hh[:, j], wring[:, w, 2 * DM:2 * DM + DM], start=True, stop=True).then_inc(ye_ok, 1)

            def quad(Q):
                for j4 in range(4):
                    tile_slot(4 * Q + j4, Q, j4)

            def quad_sum(Q, g=None):
                for j4 in range(4):
                    tile_slot(4 * Q + j4, Q, j4)
                    if j4 == 1:
                        sum_pair(Q - 1, g)

            def sum_pair(r, g=None):
                pe.wait_ge(hp_ok, r + 2)
                if g is not None:
                    pe.wait_ge(y_out, g + 1)
                nc.tensor.matmul(Y_ACC[:], ident[:], hp[:], start=(g is not None), stop=True,
                                 skip_group_check=True).then_inc(acc_ok, 2)

            quad(0)
            with pe.Fori(G1, G2 - 1) as g:
                quad_sum((g - G1) * QG + 1, g)
                with pe.Fori(2, QG + 1) as q:
                    quad_sum((g - G1) * QG + q)
            quad_sum((G2 - 1 - G1) * QG + 1, G2 - 1)
            with pe.Fori((G2 - 1 - G1) * QG + 2, (G2 - G1) * QG) as Q:
                quad_sum(Q)
            sum_pair((G2 - G1) * QG - 1)
            down(TILES, 0, 2)
            pe.wait_ge(xc_ok, TILES + C)
            pe.wait_ge(ld_res, 16)

            for i in range(8):
                sum_states(G2, i, i % 2, i == 0)
            with pe.Fori(0, 2) as h:
                for c in range(4):
                    g, q, t = G2 + h + c // 2, (c + 2) % 4, 4 * h + c
                    for i in range(4):
                        sum_states(g, 4 * q + i, i % 2, q + i == 0)
                        if i == 0:
                            pe.wait_ge(cb_out, t + 1)
                            nc.tensor.matmul(COMB[c % 2][:, 0:DM], ident[:], at(x_sb, t), start=True, stop=False)
                            pe.wait_ge(g_ld[c], h * 16 * K + 16 * K)
                        for k in (2 * i, 2 * i + 1):
                            pe.wait_ge(dg_ok, t * K + k + 1)
                            nc.tensor.matmul(COMB[c % 2][:, 0:DM], diag[:, k], rows[c][:, k], start=False,
                                             stop=(k == K - 1)).then_inc(cb_ok, 1)

            def project_out(i, ks):
                for t in range(*PARTS[i]):
                    b, c = t // (L // P), t % (L // P)
                    for k in ks:
                        mm = nc.tensor.matmul(OUT[i][:, (t - PARTS[i][0]) * DM:(t - PARTS[i][0] + 1) * DM],
                                              u[:, b, k, c * P:(c + 1) * P], wout[:, k], start=(k == 0), stop=(k == DT - 1))
                if ks[-1] == DT - 1:
                    mm.then_inc(o_ps, 1)

            pe.wait_ge(ld_wout, 16)
            pe.wait_ge(yz_ok, DT)
            for n in range(NS // 2, NS):
                sum_states(G3, n, n % 2, False)
                if n in (8, 10):
                    project_out((n - 8) // 2, range(DT))
                elif n >= 12:
                    pe.wait_ge(yz_ok, G3)
                    pe.wait_ge(cb_out, NT + 2)
                    if n >= 14:
                        pe.wait_ge(fin, n - 13)
                    project_out(n - 10, range(DT - 1))
            pe.wait_ge(yz_ok, G)
            for i in range(2, len(PARTS)):
                project_out(i, [DT - 1])


def kernel(**inputs):
    import numpy as np
    import concourse.bacc as bacc
    from concourse.bass_utils import run_bass_kernel_spmd as run

    a = {k: np.asarray(v) for k, v in inputs.items()}
    x = a["L0_attn_hidden_states"].reshape(T, DM)
    par = np.concatenate([a["L0_attn_conv_w"], a["L0_attn_conv_b"][:, None], a["L0_attn_dt_proj_b"][:, None],
                          a["L0_attn_D"][:, None], a["L0_attn_A_log"]], axis=1)
    w13 = a["L0_ffn_w13"].transpose(0, 2, 1)
    w13 = w13.reshape(E, KD, P, 2 * INTER).transpose(0, 2, 1, 3).reshape(E, P, KD * 2 * INTER)
    w_moe = np.concatenate([w13, a["L0_ffn_w2"].transpose(0, 2, 1)], axis=2)
    arrays = {
        "x": x, "w_in": a["L0_attn_in_proj_w"].T, "par": par, "w_x": a["L0_attn_x_proj_w"].T,
        "w_dt": a["L0_attn_dt_proj_w"].T, "w_out": a["L0_attn_out_proj_w"].T, "w_gate": a["L0_ffn_gate_w"].T,
        "w_moe": w_moe,
    }
    arrays = {k: np.ascontiguousarray(v) for k, v in arrays.items()}
    nc = bacc.Bacc("TRN2", target_bir_lowering=False, num_devices=1)
    args = [nc.dram_tensor(k, v.shape, F32, kind="ExternalInput").ap() for k, v in arrays.items()]
    out = nc.dram_tensor("out", (T, DM), F32, kind="ExternalOutput").ap()
    bc_dram = nc.dram_tensor("bc_dram", (2 * NS, T), F32).ap()
    slot_x = nc.dram_tensor("slot_x", (TILES * P, DM), F32).ap()
    slot_y = nc.dram_tensor("slot_y", ((TILES + 1) * P, DM), F32).ap()
    program(nc, *args, out, bc_dram, slot_x, slot_y)
    r = run(nc, [arrays], core_ids=[0])
    return r.results[0]["out"].reshape(B, L, DM)
```

```python
from contextlib import ExitStack

import concourse.bass as bass
from concourse import mybir

F32 = mybir.dt.float32
BF16 = mybir.dt.bfloat16
I32 = mybir.dt.int32
U32 = mybir.dt.uint32
ALU = mybir.AluOpType
ACT = mybir.ActivationFunctionType
AX = mybir.AxisListType

P = 128
B, L, DM = 2, 512, 256
DI, NS, DC, R = 512, 16, 4, 128
E, K, INTER = 64, 8, 128
T = B * L
NT = T // P
KD = DM // P
DT = DI // P
G = B * DT
UNITS = G * NS
TILES = T * K // P + E
WGU = KD * 2 * INTER
WCOL = WGU + DM
LAG = 3
EPS = 1e-5
C = 2
CW, CB, DTB, DSKIP, ALOG, NPAR = 0, DC, DC + 1, DC + 2, DC + 3, DC + 3 + NS

assert UNITS == P and TILES == 128 and NT == G and L == 512 and DM == 2 * P and 2 * INTER == DM


def program(nc, x, w_in, par, w_x, w_dt, w_out, w_gate, w_moe, out, bc_dram, slot_x, slot_y):
    with ExitStack() as ctx:
        def sb(name, shape, dt=F32):
            return ctx.enter_context(nc.sbuf_tensor(name, shape, dt))

        def sem(name):
            return ctx.enter_context(nc.semaphore(name))

        x_sb = sb("x_sb", [P, NT, DM])
        xT = sb("xT", [P, KD, T])
        win = sb("win", [P, KD, 2 * DI])
        xpad = sb("xpad", [P, B, DT, L + DC - 1])
        u = sb("u", [P, B, DT, L])
        dt_sb = sb("dt_sb", [P, G, L])
        dtu = sb("dtu", [P, G, L])
        bc = sb("bc", [P, NS, 2, L])
        wring = sb("wring", [P, 4, WCOL])
        prob = sb("prob", [P, NT, E])
        mask = sb("mask", [P, NT, E])
        key = sb("key", [P, NT, E])
        dA = sb("dA", [P, 2, L])
        dbu = sb("dbu", [P, 2, L])
        hc = sb("hc", [P, 2, L])
        wx = sb("wx", [P, DT, R + 3 * 2 * NS])
        parts = sb("parts", [3 * 2 * NS, L], BF16)
        pick = sb("pick", [3 * 2 * NS, 2 * NS], BF16)
        wdt = sb("wdt", [P, DI])
        wout = sb("wout", [P, DT, DM])
        wgate = sb("wgate", [P, KD, E])
        ident = sb("ident", [P, P])
        ones = sb("ones", [P, P])
        tri = sb("tri", [E, E])
        thr = sb("thr", [E, 8])
        tau = sb("tau", [E, TILES])
        pars = sb("pars", [P, DT, NPAR])
        a_neg = sb("a_neg", [P, G, NS])
        a_pos = sb("a_pos", [P, DT, NS])
        d_col = sb("d_col", [P, G, 1])
        dtb2 = sb("dtb2", [P, DT, 1])
        stats = sb("stats", [P, NT, 6])
        mv = sb("mv", [P, NT, 2])
        ve = sb("ve", [P, NT])
        sd = sb("sd", [P, NT])
        rstd = sb("rstd", [P, NT])
        mx = sb("mx", [P, NT])
        sm = sb("sm", [P, NT])
        rs = sb("rs", [P, NT])
        m8 = sb("m8", [P, NT, K])
        k8 = sb("k8", [P, NT, K])
        c8 = sb("c8", [P, NT, K])
        slot = sb("slot", [P, NT * K], U32)
        slot_r = sb("slot_r", [P, NT * K], U32)
        n_tile = sb("n_tile", [E, 1])
        n_junk = sb("n_junk", [E, 8])
        base = sb("base", [E, 1])
        upto = sb("upto", [E, 1])
        tile_e = sb("tile_e", [1, TILES], I32)
        xg = sb("xg", [P, 2, 2, DM])
        th = sb("th", [P, 2, INTER])
        gt = sb("gt", [P, INTER])
        hp = sb("hp", [P, L])
        PS = [ctx.enter_context(nc.psum_tensor(f"bank{i}", [P, 512], F32)) for i in range(8)]

        zeros = bc[:, 0:2].rearrange("p a b l -> p (a b l)")
        wflat = wring[0:E].rearrange("p a b -> p (a b)")
        cum, cmp = wflat[:, 0:T], wflat[:, T:T + TILES]
        bcs = dbu
        dtr = hc
        xpad_f = xpad[:].rearrange("p b d l -> p (b d l)")[:, 0:G * L].rearrange("p (g l) -> p g l", g=G)
        sp_e = xpad_f
        z_sb = xpad_f
        sp_l = dtu
        hh = wdt[:].rearrange("p (a i) -> p a i", a=4)
        c8_junk = mask
        rest = hp
        xTs = x_sb[:, 0:2]
        ysb = x_sb[:, 2:6].rearrange("p (a b) d -> p a b d", a=2)
        diag = wring[:].rearrange("p a b -> p (a b)")[:, 0:K * P].rearrange("p (k q) -> p k q", k=K)
        u_g = u[:].rearrange("p b d l -> p (b d) l")
        rows = [xT[:].rearrange("p k t -> p (k t)").rearrange("p (k d) -> p k d", k=K),
                win[:].rearrange("p k e -> p (k e)").rearrange("p (k d) -> p k d", k=K),
                dt_sb[:, 0:DT].rearrange("p g l -> p (g l)").rearrange("p (k d) -> p k d", k=K),
                dtu[:, 0:DT].rearrange("p g l -> p (g l)").rearrange("p (k d) -> p k d", k=K)]
        free = [xT[:].rearrange("p k t -> p (k t)"), win[:].rearrange("p k e -> p (k e)")]
        w_buf = [wring[:, i] for i in range(4)] + [f[:, i * WCOL:(i + 1) * WCOL] for f in free for i in range(2)]
        x_buf = [xg[:, 0], xg[:, 1]] + [f[:, 2 * WCOL:2 * WCOL + 2 * DM].rearrange("p (j d) -> p j d", j=2) for f in free]
        Y_ACC, ROW, H, XT, GU, YT = PS[0], [PS[1], PS[2]], PS[3], PS[4], [PS[5], PS[6]], PS[7]
        OUT = [PS[i][:, 0:DM] for i in (4, 5, 6, 7, 1, 2, 4, 5)]

        ld_x, ld_x1, ld_gate, ld_in, ld_par, ld_wx, ld_wdt, ld_wout = map(
            sem, "ld_x ld_x1 ld_gate ld_in ld_par ld_wx ld_wdt ld_wout".split())
        consts, zset = sem("consts"), sem("zset")
        zeroed = sem("zeroed")
        ln, sd_ready = sem("ln"), sem("sd_ready")
        xt_ps, xt_ready = sem("xt_ps"), sem("xt_ready")
        pe_r, rt, ac_r = sem("pe_r"), sem("rt"), sem("ac_r")
        in_ps, in_ready, in_tap = sem("in_ps"), sem("in_ready"), sem("in_tap")
        conv = [sem(f"conv{d}") for d in range(DT)]
        u_ready = sem("u_ready")
        bc_ps, bc_row, bc_st = map(sem, "bc_ps bc_row bc_st".split())
        bc_ld = [sem(f"bc_ld{q}") for q in range(NS // 4)]
        split, picked = sem("split"), sem("picked")
        row_ps = [sem("row_ps0"), sem("row_ps1")]
        row_ok = [sem("row_ok0"), sem("row_ok1")]
        dr_ps, dr_ready = sem("dr_ps"), sem("dr_ready")
        dt_ps, dt_abs, dt_max = sem("dt_ps"), sem("dt_abs"), sem("dt_max")
        sp_x, sp_s, sp_c, sp_ln, sp_v, a_exp, small = map(sem, "sp_x sp_s sp_c sp_ln sp_v a_exp small".split())
        scat, ld_res = sem("scat"), sem("ld_res")
        dA_ok, dbu_ok, dbv_ok, scan_ok, hc_ok, hp_ok, acc_ok, y_out, yz_ok = map(
            sem, "dA_ok dbu_ok dbv_ok scan_ok hc_ok hp_ok acc_ok y_out yz_ok".split())
        xg_ld = [sem(f"xg_ld{i}") for i in range(4)]
        w_ld = [sem(f"w_ld{i}") for i in range(8)]
        y_st = [sem("y_st0"), sem("y_st1")]
        t_ok, xc_ok, gu_ok, th_ok, gt_ok, hh_ok, ye_ok, yc_ok = map(
            sem, "t_ok xc_ok gu_ok th_ok gt_ok hh_ok ye_ok yc_ok".split())
        tick = sem("tick")
        g_ld = [sem(f"g_ld{i}") for i in range(4)]
        z_ps, z_ok, c8_ok = map(sem, "z_ps z_ok c8_ok".split())
        dg_ok, cb_ok, cb_out, o_ps, fin, o_st = map(sem, "dg_ok cb_ok cb_out o_ps fin o_st".split())

        x_t = x.rearrange("(t p) d -> p t d", p=P)
        out_t = out.rearrange("(t p) d -> p t d", p=P)
        slot_x_t = slot_x.rearrange("(i j p) d -> i p j d", j=2, p=P)
        slot_y_t = slot_y.rearrange("(i j p) d -> i p j d", j=2, p=P)
        bc_v = bc_dram.rearrange("(c n) l -> c n l", c=2)
        CONSTS = 6
        RT_SUB, RT_PROB, RT_MAX, RT_REP, RT_MASK = 2, 5, 5 + NT, 5 + 2 * NT, 6 + 2 * NT
        RT_CUM0, RT_CUM, RT_NT, RT_BASE, RT_UPTO, RT_POS, RT_CMP, RT_KEY = range(RT_MASK + 1, RT_MASK + 9)
        RT_K8 = RT_KEY + NT
        RT_SLOT, RT_SLOT1, RT_TILE = RT_K8 + 1, RT_K8 + 2, RT_K8 + 3
        SP_STEPS = 3
        G1, GH, G2, G3 = 1, DT - 1, G - 2, G - 1
        QG = NS // 2
        LIGHT = 3 * QG
        V_HEAVY, V_LAST = (GH - G1) * LIGHT, (GH - G1) * LIGHT + 4 * QG
        assert V_LAST + (G2 - GH - 1) * LIGHT == TILES
        ZERO_DMAS = 16
        PROJ = {9: (4, 0), 11: (4, 1), 13: (5, 0), 15: (5, 1), 17: (6, 0), 19: (6, 1), 21: (7, 0), 23: (7, 1),
                25: (6, 2), 27: (7, 2), 29: (4, 2), 30: (5, 2)}
        block = ctx.enter_context(nc.Block())

        def at(t, i):
            return t[:, bass.ds(i, 1)].rearrange("p a l -> p (a l)")

        @block.sync
        def _(sp):
            sp.dma_start(x_sb[:, 0:NT // 2], x_t[:, 0:NT // 2]).then_inc(ld_x, 16)
            sp.dma_start(x_sb[:, NT // 2:NT], x_t[:, NT // 2:NT]).then_inc(ld_x1, 16)
            sp.dma_start(wgate[:], w_gate.rearrange("(k p) e -> p k e", p=P)).then_inc(ld_gate, 16)
            sp.dma_start(win[:], w_in.rearrange("(k p) e -> p k e", p=P)).then_inc(ld_in, 16)
            sp.dma_start(pars[:], par.rearrange("(t p) n -> p t n", p=P)).then_inc(ld_par, 16)
            sp.wait_ge(zset, 1)
            n = TILES * P // ZERO_DMAS
            for i in range(ZERO_DMAS):
                sp.dma_start(slot_x[i * n:(i + 1) * n].rearrange("(p r) d -> p (r d)", p=P), zeros).then_inc(zeroed, 16)
                if i == 0:
                    sp.dma_start(wx[:], w_x.rearrange("(t p) n -> p t n", p=P)).then_inc(ld_wx, 16)
                    sp.dma_start(wdt[:], w_dt).then_inc(ld_wdt, 16)
            sp.dma_start(wout[:], w_out.rearrange("(t p) n -> p t n", p=P)).then_inc(ld_wout, 16)
            sp.wait_ge(bc_row, 1)
            sp.dma_start(bc_dram, bcs[0:2 * NS, 0]).then_inc(bc_st, 16)
            sp.wait_ge(bc_st, 16)
            sp.wait_ge(zeroed, 16 * ZERO_DMAS)
            sp.wait_ge(rt, RT_CUM)
            for q in range(NS // 4):
                for c in range(2):
                    sp.dma_start(bc[:, 4 * q:4 * q + 4, c], bc_v[c, 4 * q:4 * q + 4].partition_broadcast(P)).then_inc(bc_ld[q], 16)
            sp.wait_ge(rt, RT_TILE)
            for j in range(2):
                sp.sem_inc(y_st[j], 16)
            sp.sem_inc(w_ld[7], 16)

            def load_w(v, j, wait=True):
                e = sp.value_load(tile_e[0:1, bass.ds(v, 1)], min_val=0, max_val=E - 1)
                if wait:
                    sp.wait_ge(ye_ok, v - 8 + LAG + 1 + C)
                sp.dma_start(w_buf[j], w_moe[bass.ds(e, 1)].rearrange("a p n -> p (a n)")).then_inc(w_ld[j], 16)

            def load_x(i, j):
                sp.dma_start(x_buf[j], slot_x_t[bass.ds(i, 1)].rearrange("a p j d -> p (a j) d")).then_inc(xg_ld[j], 16)

            def store_y(i, j):
                sp.dma_start(slot_y_t[bass.ds(i, 1)].rearrange("a p j d -> p (a j) d"), ysb[:, j]).then_inc(y_st[j], 16)

            for i in range(4):
                load_w(i, i, False)
            sp.wait_ge(z_ps, G)
            load_w(4, 4, False)
            sp.wait_ge(scat, 16 * NT * K)
            for i in range(4):
                load_x(i, i)

            def octet(O, last=False):
                for i in range(8):
                    if not last or i < 2:
                        load_w(8 * O + 5 + i, (5 + i) % 8)
                    if i % 2 and not last:
                        sp.wait_ge(t_ok, 8 * O + i + 1)
                        load_x(4 * O + 4 + i // 2, i // 2)
                    if i % 2:
                        sp.wait_ge(yc_ok, 8 * O + i + 1 + C)
                        store_y(4 * O + i // 2, i // 2 % 2)

            with sp.Fori(0, TILES // 8 - 1) as O:
                octet(O)
            octet(TILES // 8 - 1, last=True)
            sp.wait_ge(yc_ok, TILES + 2 + C)
            store_y(TILES // 2, 0)
            sp.wait_ge(gu_ok, TILES + C)
            for j in range(2):
                sp.wait_ge(y_st[j], 16 * (TILES // 4) + 16 + (16 if j == 0 else 0))
            sp.dma_start(x_sb[:], x_t).then_inc(ld_res, 16)
            for t in range(NT):
                if t < NT - 1:
                    sp.wait_ge(cb_out, t + 1)
                else:
                    sp.wait_ge(fin, K + 1)
                sp.dma_start(out_t[:, t], x_sb[:, t]).then_inc(o_st, 16)
            sp.wait_ge(o_st, 16 * NT)

        @block.gpsimd
        def _(pool):
            nc.gpsimd.memset(zeros, 0.0).then_inc(zset, 1)
            nc.gpsimd.memset(ones[:], 1.0).then_inc(consts, 1)
            nc.gpsimd.memset(xpad[:, :, :, 0:DC - 1], 0.0).then_inc(consts, 1)
            nc.gpsimd.iota(thr[:], [[P, 8]], base=0, channel_multiplier=0,
                           allow_small_or_imprecise_dtypes=True).then_inc(consts, 1)
            nc.gpsimd.iota(tau[:], [[1, TILES]], base=0, channel_multiplier=0,
                           allow_small_or_imprecise_dtypes=True).then_inc(consts, 1)
            pool.wait_ge(consts, 4)
            nc.gpsimd.affine_select(out=ident[:], in_=ones[:], compare_op=ALU.is_equal, fill=0.0, base=0,
                                    pattern=[[-1, P]], channel_multiplier=1).then_inc(consts, 1)
            nc.gpsimd.affine_select(out=tri[:], in_=ones[0:E, 0:E], compare_op=ALU.is_gt, fill=0.0, base=0,
                                    pattern=[[1, E]], channel_multiplier=-1).then_inc(consts, 1)
            pool.wait_ge(consts, CONSTS)
            pool.wait_ge(rt, RT_SLOT)
            pool.wait_ge(zeroed, 16 * ZERO_DMAS)
            for t in range(NT):
                for k in range(K):
                    pool.indirect_dma_start(
                        slot_x, bass.IndirectOffsetOnAxis(ap=slot[:, t * K + k:t * K + k + 1], axis=0),
                        x_sb[:, t, :], None).then_inc(scat, 16)

            def spread_u(g, n, j):
                pool.wait_ge(scan_ok, g * NS + n + C - 1)
                pool.sem_inc(tick, 1)
                nc.gpsimd.tensor_tensor(dbu[:, j], at(dtu, g), bc[:, bass.ds(n, 1), 0].rearrange(
                    "p a l -> p (a l)"), ALU.mult).then_inc(dbu_ok, 1)

            def add_pair(r):
                pool.wait_ge(hc_ok, G1 * NS + 2 * r + 2 + C)
                pool.wait_ge(acc_ok, G1 * NS + 2 * r + C)
                nc.gpsimd.tensor_tensor(hp[:], hc[:, 0], hc[:, 1], ALU.add).then_inc(hp_ok, 1)

            def pair(g, q):
                for j in range(2):
                    spread_u(g, 2 * q + j, j)
                add_pair((g - G1) * QG + q - 1)

            with pool.Fori(G1, DT) as g:
                with pool.Fori(0, QG) as q:
                    pair(g, q)
            pool.wait_ge(row_ok[0], NS + 1)
            with pool.Fori(DT, G2) as g:
                with pool.Fori(0, QG) as q:
                    pair(g, q)
            add_pair((G2 - G1) * QG - 1)
            pool.wait_ge(y_st[0], 16 * (TILES // 4 + 1) + 16)
            pool.wait_ge(y_st[1], 16 * (TILES // 4) + 16)
            pool.wait_ge(z_ps, G)
            pool.wait_ge(dA_ok, DT * NS)
            pool.wait_ge(dbu_ok, (DT - 1) * NS)
            pool.wait_ge(dbv_ok, NS)
            for t in range(NT):
                if t >= 4:
                    pool.wait_ge(cb_ok, K * (t - 2))
                for k in range(K):
                    pool.indirect_dma_start(
                        rows[t % 4][:, k, :], None, slot_y,
                        bass.IndirectOffsetOnAxis(ap=slot_r[:, t * K + k:t * K + k + 1], axis=0)).then_inc(g_ld[t % 4], 16)

        @block.vector
        def _(dve):
            def conv_block(d):
                dve.wait_ge(in_ready, 2 * d + 2)
                dve.wait_ge(in_tap, 2 * d + 2)
                for j in range(DC - 1):
                    if j:
                        dve.wait_ge(conv[d], j)
                    nc.vector.scalar_tensor_tensor(u[:, :, d], xpad[:, :, d, j:j + L], pars[:, d, CW + j:CW + j + 1],
                                                   u[:, :, d], ALU.mult, ALU.add).then_inc(conv[d], 1)

            for t in range(NT):
                if t % (NT // 2) == 0:
                    dve.wait_ge([ld_x, ld_x1][t // (NT // 2)], 16)
                nc.vector.bn_stats(stats[:, t], x_sb[:, t]).then_inc(ln, 1)
            dve.wait_ge(ln, NT)
            for t in range(NT):
                nc.vector.bn_aggr(mv[:, t], stats[:, t]).then_inc(ln, 1)
            dve.wait_ge(ln, 2 * NT)
            nc.vector.tensor_scalar(ve[:], mv[:, :, 1], EPS, None, ALU.add).then_inc(ln, 1)
            dve.wait_ge(sd_ready, 1)
            nc.vector.reciprocal(rstd[:], sd[:]).then_inc(ln, 1)
            dve.wait_ge(ln, 2 * NT + 2)
            for t in range(NT):
                nc.vector.tensor_scalar(x_sb[:, t], x_sb[:, t], mv[:, t, 0:1], rstd[:, t:t + 1],
                                        ALU.subtract, ALU.mult).then_inc(ln, 1)
            for h in range(2):
                dve.wait_ge(xt_ps, 2 * h + 1)
                nc.vector.tensor_copy(xT[:, 0, h * 512:(h + 1) * 512], PS[2 * h][:]).then_inc(xt_ready, 1)
            logit = PS[4][:].rearrange("p (t e) -> p t e", t=NT)
            dve.wait_ge(pe_r, 1)
            nc.vector.tensor_reduce(mx[:], logit, AX.X, ALU.max).then_inc(rt, 1)
            dve.wait_ge(rt, 1)
            nc.vector.tensor_tensor(prob[:], logit, mx[:].unsqueeze(2).broadcast_to([P, NT, E]), ALU.subtract).then_inc(rt, 1)
            dve.wait_ge(ac_r, 1)
            nc.vector.tensor_reduce(sm[:], prob[:], AX.X, ALU.add).then_inc(rt, 1)
            dve.wait_ge(rt, 3)
            nc.vector.reciprocal(rs[:], sm[:]).then_inc(rt, 1)
            dve.wait_ge(rt, 4)
            nc.vector.tensor_tensor(prob[:], prob[:], rs[:].unsqueeze(2).broadcast_to([P, NT, E]), ALU.mult).then_inc(rt, 1)
            dve.wait_ge(rt, RT_PROB)
            for t in range(NT):
                nc.vector.max(m8[:, t], prob[:, t]).then_inc(rt, 1)
            dve.wait_ge(rt, RT_MAX)
            for t in range(NT):
                nc.vector.match_replace(mask[:, t], m8[:, t], prob[:, t], -1.0).then_inc(rt, 1)
            dve.wait_ge(rt, RT_REP)
            nc.vector.tensor_scalar(mask[:], mask[:], 0.0, None, ALU.is_lt).then_inc(rt, 1)
            dve.wait_ge(ld_par, 16)
            dve.wait_ge(consts, CONSTS)
            conv_block(0)
            dve.wait_ge(pe_r, 2)
            dve.wait_ge(zset, 1)
            zrow = zeros[0:E, 0:512]
            nc.vector.tensor_tensor_scan(cum[:, 0:512], zrow, PS[5][0:E, :], 0.0, ALU.add, ALU.add).then_inc(rt, 1)
            dve.wait_ge(rt, RT_CUM0)
            nc.vector.tensor_tensor_scan(cum[:, 512:1024], zrow, PS[6][0:E, :], cum[:, 511:512], ALU.add, ALU.add).then_inc(rt, 1)
            dve.wait_ge(rt, RT_CUM)
            nc.vector.tensor_scalar(n_junk[:], thr[:], cum[:, T - 1:T], None, ALU.is_lt, ALU.add,
                                    accum_out=n_tile[:]).then_inc(rt, 1)
            dve.wait_ge(pe_r, 3)
            nc.vector.tensor_scalar(base[:], PS[4][0:E, 0:1], float(P), None, ALU.mult).then_inc(rt, 1)
            dve.wait_ge(rt, RT_NT)
            nc.vector.tensor_tensor(upto[:], PS[4][0:E, 0:1], n_tile[:], ALU.add).then_inc(rt, 1)
            dve.wait_ge(rt, RT_BASE)
            nc.vector.tensor_scalar(cum, cum, base[:], None, ALU.add).then_inc(rt, 1)
            dve.wait_ge(rt, RT_UPTO)
            nc.vector.tensor_scalar(cmp, tau[:], upto[:], None, ALU.is_ge).then_inc(rt, 1)
            dve.wait_ge(pe_r, 4)
            nc.vector.tensor_tensor(key[:].rearrange("p t e -> p (t e)"), mask[:].rearrange("p t e -> p (t e)"),
                                    PS[7][:], ALU.mult).then_inc(rt, 1)
            dve.wait_ge(rt, RT_KEY)
            for t in range(NT):
                nc.vector.max(k8[:, t], key[:, t]).then_inc(rt, 1)
            dve.wait_ge(rt, RT_K8)
            k8f = k8[:].rearrange("p t k -> p (t k)")
            nc.vector.tensor_scalar(slot[:], k8f, -1.0, None, ALU.add).then_inc(rt, 1)
            nc.vector.tensor_scalar(slot_r[:], k8f, float(LAG * P - 1), None, ALU.add).then_inc(rt, 1)
            dve.wait_ge(pe_r, 5)
            nc.vector.tensor_scalar(tile_e[:], PS[4][0:1, P:P + TILES], float(E - 1), None, ALU.min).then_inc(rt, 1)
            for d in range(1, DT):
                conv_block(d)
            nc.vector.tensor_tensor(pick[:], ident[0:3 * 2 * NS, 0:2 * NS], ident[0:3 * 2 * NS, 2 * NS:2 * 2 * NS], ALU.add).then_inc(picked, 1)
            dve.wait_ge(a_exp, 1)
            for b in range(B):
                nc.vector.tensor_scalar(a_neg[:, b * DT:(b + 1) * DT], a_pos[:], -1.0, None, ALU.mult).then_inc(small, 1)
                nc.vector.tensor_copy(d_col[:, b * DT:(b + 1) * DT], pars[:, :, DSKIP:DSKIP + 1]).then_inc(small, 1)
            nc.vector.tensor_scalar(dtb2[:], pars[:, :, DTB:DTB + 1], 2.0, None, ALU.mult).then_inc(small, 1)
            dve.wait_ge(small, 5)
            dve.wait_ge(picked, 1)
            nc.vector.tensor_tensor(pick[:], pick[:], ident[0:3 * 2 * NS, 2 * 2 * NS:3 * 2 * NS], ALU.add).then_inc(picked, 1)
            dve.wait_ge(split, 1)
            nc.vector.tensor_tensor(rest[0:3 * 2 * NS], PS[3][0:3 * 2 * NS, :], parts[:], ALU.subtract).then_inc(split, 1)
            dve.wait_ge(split, 2)
            for i in range(1, 3):
                lo = slice(i * 2 * NS, (i + 1) * 2 * NS)
                nc.vector.tensor_copy(parts[lo], rest[lo]).then_inc(split, 1)
            dve.wait_ge(split, 4)
            nc.vector.tensor_tensor(parts[lo], rest[lo], parts[lo], ALU.subtract).then_inc(split, 1)

            def over_zero(g):
                dve.wait_ge(dt_abs, g + 1)
                nc.vector.tensor_scalar(dt_sb[:, g], PS[4 + g % 4][:], dtb2[:, g % DT], 0.0, ALU.add, ALU.max).then_inc(dt_max, 1)

            def rounded(g):
                dve.wait_ge(sp_s, g + 1)
                nc.vector.scalar_tensor_tensor(sp_e[:, g], sp_l[:, g], -1.0, sp_e[:, g], ALU.add, ALU.subtract).then_inc(sp_c, 1)

            def softplus(g):
                dve.wait_ge(sp_ln, g + 1)
                nc.vector.tensor_tensor(sp_l[:, g], sp_l[:, g], sp_e[:, g], ALU.subtract).then_inc(sp_v, 1)
                dve.wait_ge(sp_v, SP_STEPS * g + 1)
                nc.vector.tensor_tensor(dt_sb[:, g], dt_sb[:, g], sp_l[:, g], ALU.add).then_inc(sp_v, 1)
                dve.wait_ge(sp_v, SP_STEPS * g + 2)
                nc.vector.tensor_tensor(dtu[:, g], dt_sb[:, g], u_g[:, g], ALU.mult).then_inc(sp_v, 1)

            for g in range(G):
                over_zero(g)
                if g:
                    rounded(g - 1)
            rounded(G - 1)
            dve.wait_ge(dt_max, G)
            for g in range(G):
                softplus(g)
            dve.wait_ge(sp_v, SP_STEPS * G)
            for s_ in (scan_ok, hc_ok, hh_ok):
                dve.sem_inc(s_, C)
            dve.sem_inc(y_out, 1)

            def spread_u(g, n, j):
                dve.wait_ge(scan_ok, g * NS + n + C - 1)
                nc.vector.tensor_tensor(dbu[:, j], at(dtu, g), bc[:, bass.ds(n, 1), 0].rearrange("p a l -> p (a l)"),
                                        ALU.mult).then_inc(dbv_ok, 1)

            def scan(g, n, j):
                s = g * NS + n
                dve.wait_ge(dA_ok, s + 1)
                dve.wait_ge(hc_ok, s + C)
                nc.vector.tensor_tensor_scan(H[:], dA[:, j], dbu[:, j], 0.0, ALU.mult, ALU.add).then_inc(scan_ok, 1)

            def times_c(g, n, j, alone=True):
                s = g * NS + n
                if alone:
                    dve.wait_ge(acc_ok, s + C - 1)
                dve.wait_ge(scan_ok, s + C + 1)
                nc.vector.tensor_tensor(hc[:, j], H[:], bc[:, bass.ds(n, 1), 1].rearrange("p a l -> p (a l)"),
                                        ALU.mult).then_inc(hc_ok, 1)

            def finish_group(g):
                dve.wait_ge(acc_ok, (g + 1) * NS + C)
                nc.vector.scalar_tensor_tensor(at(u_g, g), at(u_g, g), at(d_col, g), Y_ACC[:], ALU.mult, ALU.add).then_inc(y_out, 1)
                dve.wait_ge(y_out, g + 2)
                nc.vector.tensor_tensor(at(u_g, g), at(u_g, g), at(z_sb, g), ALU.mult).then_inc(yz_ok, 1)

            def hidden(v, j4):
                j, w = (j4 + 1) % 2, (j4 + 3) % 4
                dve.wait_ge(th_ok, v + 1)
                dve.wait_ge(hh_ok, v + C)
                nc.vector.scalar_tensor_tensor(gt[:], th[:, j], 1.0, GU[j][:, 0:INTER], ALU.add, ALU.mult).then_inc(gt_ok, 1)
                dve.wait_ge(ye_ok, v - 1 + C)
                dve.wait_ge(gt_ok, v + 1)
                nc.vector.scalar_tensor_tensor(hh[:, w], gt[:], 0.5, GU[j][:, INTER:2 * INTER],
                                               ALU.mult, ALU.mult).then_inc(hh_ok, 1)

            def pair0(g, q, count, after=None):
                for j in range(2):
                    n = 2 * q + j
                    dve.wait_ge(dbv_ok, count + n + 1)
                    scan(g, n, j)
                    if j == 0 or after is None:
                        spread_u(g, n + 1, 1 - j)
                    elif len(after):
                        spread_u(after[0], 0, 0)
                    times_c(g, n, j)

            for q in range(NS // 4):
                dve.wait_ge(bc_ld[q], 32)
                if q == 0:
                    spread_u(0, 0, 0)
                    pair0(0, 0, 0)
                else:
                    pair0(0, 2 * q - 1, 0)
                    pair0(0, 2 * q, 0)
            pair0(0, QG - 1, 0, ())

            def unit(g, q, j, tiles, weights, ready=True):
                n, r = 2 * q + j, (g - G1) * QG + q
                dve.wait_ge(dbu_ok, (g - G1) * NS + n + 1)
                scan(g, n, j)
                hidden(*tiles[0])
                if j == 0:
                    dve.wait_ge(hp_ok, r + 1)
                times_c(g, n, j, False)
                if len(tiles) == 2:
                    hidden(*tiles[1])
                for i, k in enumerate(weights):
                    nc.vector.scalar_tensor_tensor(
                        c8_junk[:, 2 * j + i], at(key, q), k8[:, bass.ds(q, 1), bass.ds(k, 1)].rearrange("p a b -> p (a b)"),
                        at(prob, q), ALU.is_equal, ALU.mult,
                        accum_out=c8[:, bass.ds(q, 1), bass.ds(k, 1)].rearrange("p a b -> p (a b)")).then_inc(c8_ok, 1)

            def light(g, v, weights):
                for c in range(4):
                    unit(g, c, 0, [(v + 3 * c, 3 * c % 4), (v + 3 * c + 1, (3 * c + 1) % 4)], weights[0])
                    unit(g, c, 1, [(v + 3 * c + 2, (3 * c + 2) % 4)], weights[1])
                    if c == 0:
                        finish_group(g - 1)
                for c in range(4, QG):
                    unit(g, c, 0, [(v + 3 * c, 3 * c % 4), (v + 3 * c + 1, (3 * c + 1) % 4)], weights[0])
                    unit(g, c, 1, [(v + 3 * c + 2, (3 * c + 2) % 4)], weights[1])

            def row_c(m):
                dve.wait_ge(row_ps[1], m + 1)
                dve.wait_ge(hc_ok, (DT - 1) * NS + m + 1 + C)
                nc.vector.tensor_copy(bc[:, bass.ds(m, 1), 1].rearrange("p a l -> p (a l)"), ROW[1][:]).then_inc(row_ok[1], 1)

            def heavy(q, rows):
                v = V_HEAVY + 4 * q
                for j in range(2):
                    unit(GH, q, j, [(v + 2 * j, 2 * j), (v + 2 * j + 1, 2 * j + 1)], (4 + 2 * j, 5 + 2 * j))
                    if rows:
                        row_c(2 * q + j - 2)

            dve.wait_ge(z_ok, G)
            with dve.Fori(G1, GH) as g:
                light(g, (g - G1) * LIGHT, [((g - G1) * 2,), ((g - G1) * 2 + 1,)])
            heavy(0, False)
            finish_group(GH - 1)
            with dve.Fori(1, QG) as q:
                heavy(q, True)
            for m in range(NS - 2, NS):
                row_c(m)
            dve.wait_ge(row_ok[1], NS + 1)
            with dve.Fori(GH + 1, G2) as g:
                light(g, (g - GH - 1) * LIGHT + V_LAST, [(), ()])

            spread_u(G2, 0, 0)
            dve.wait_ge(hp_ok, (G2 - G1) * QG + 1)
            pair0(G2, 0, NS)
            finish_group(G2 - 1)
            with dve.Fori(1, QG - 1) as q:
                pair0(G2, q, NS)
            pair0(G2, QG - 1, NS, (G3,))
            pair0(G3, 0, 2 * NS)
            finish_group(G2)
            with dve.Fori(1, QG - 1) as q:
                pair0(G3, q, 2 * NS)
            pair0(G3, QG - 1, 2 * NS, ())
            finish_group(G3)
            t = NT - 1
            dve.wait_ge(ld_res, 16)
            dve.wait_ge(g_ld[t % 4], (t // 4 + 1) * 16 * K)
            for k in range(K):
                if k:
                    dve.wait_ge(fin, k)
                nc.vector.scalar_tensor_tensor(x_sb[:, t], rows[t % 4][:, k], c8[:, t, k:k + 1], x_sb[:, t],
                                               ALU.mult, ALU.add).then_inc(fin, 1)
            dve.wait_ge(fin, K)
            dve.wait_ge(o_ps, 4)
            nc.vector.tensor_tensor(x_sb[:, t], x_sb[:, t], OUT[t], ALU.add).then_inc(fin, 1)

        @block.scalar
        def _(act):
            act.wait_ge(ln, 2 * NT + 1)
            nc.scalar.activation(sd[:], ve[:], ACT.Sqrt).then_inc(sd_ready, 1)
            for h in range(2):
                act.wait_ge(xt_ps, 2 * h + 2)
                nc.scalar.copy(xT[:, 1, h * 512:(h + 1) * 512], PS[2 * h + 1][:]).then_inc(xt_ready, 1)
            act.wait_ge(ld_par, 16)
            nc.scalar.activation(a_pos[:], pars[:, :, ALOG:ALOG + NS], ACT.Exp).then_inc(a_exp, 1)
            act.wait_ge(rt, RT_SUB)
            nc.scalar.activation(prob[:], prob[:], ACT.Exp).then_inc(ac_r, 1)
            act.wait_ge(consts, CONSTS)
            for i in range(G):
                d, b = i // B, i % B
                act.wait_ge(in_ps, i + 1)
                nc.scalar.copy(xpad[:, b, d, DC - 1:], PS[i % 4][:]).then_inc(in_ready, 1)
                nc.scalar.activation(u[:, b, d], PS[i % 4][:], ACT.Copy, scale=pars[:, d, CW + DC - 1:CW + DC]).then_inc(in_tap, 1)
            for d in range(DT):
                act.wait_ge(conv[d], DC - 1)
                nc.scalar.activation(u[:, :, d], u[:, :, d], ACT.Silu, bias=pars[:, d, CB:CB + 1]).then_inc(u_ready, 1)
            for b in range(B):
                act.wait_ge(bc_ps, b + 1)
                if b == 0:
                    nc.scalar.copy(bcs[0:2 * NS, b], PS[2][0:2 * NS, :]).then_inc(bc_row, 1)
                else:
                    nc.scalar.copy(parts[:], PS[3][0:3 * 2 * NS, :]).then_inc(split, 1)
            for b in range(B):
                act.wait_ge(dr_ps, b + 1)
                nc.scalar.copy(dtr[:, b], PS[b][:]).then_inc(dr_ready, 1)
            act.wait_ge(small, 5)
            for g in range(G):
                act.wait_ge(dt_ps, g + 1)
                nc.scalar.activation(sp_e[:, g], PS[4 + g % 4][:], ACT.Abs, bias=dtb2[:, g % DT]).then_inc(dt_abs, 1)
                act.wait_ge(dt_abs, g + 1)
                nc.scalar.activation(sp_e[:, g], sp_e[:, g], ACT.Exp, scale=-1.0).then_inc(sp_x, 1)
                act.wait_ge(sp_x, g + 1)
                nc.scalar.activation(sp_l[:, g], sp_e[:, g], ACT.Copy, bias=1.0).then_inc(sp_s, 1)
            for g in range(G):
                act.wait_ge(sp_c, g + 1)
                nc.scalar.activation(sp_l[:, g], sp_l[:, g], ACT.Ln).then_inc(sp_ln, 1)
            for g in range(G):
                act.wait_ge(z_ps, g + 1)
                act.wait_ge(sp_v, SP_STEPS * g + 1)
                nc.scalar.copy(z_sb[:, g], PS[4 + g % 4][:]).then_inc(z_ok, 1)
            act.wait_ge(sp_v, SP_STEPS * G)
            for s_ in (xc_ok, yc_ok):
                act.sem_inc(s_, C)

            def decay(g, n, j):
                act.wait_ge(scan_ok, g * NS + n + C - 1)
                act.sem_inc(tick, 1)
                nc.scalar.activation(dA[:, j], at(dt_sb, g), ACT.Exp, scale=a_neg[:, bass.ds(g, 1), bass.ds(n, 1)].rearrange(
                    "p a l -> p (a l)")).then_inc(dA_ok, 1)

            for n in range(NS):
                decay(0, n, n % 2)

            def copies(v, Q, j4):
                j, i = j4 % 2, j4 // 2
                act.wait_ge(ye_ok, v + C + 1)
                if j == 0:
                    act.wait_ge(y_st[i], Q * 16 + 16)
                nc.scalar.copy(ysb[:, i, j], YT[:, 0:DM]).then_inc(yc_ok, 1)
                act.wait_ge(t_ok, v + 1)
                act.wait_ge(gu_ok, v + C)
                nc.scalar.copy(xTs[:, j], XT[:, 0:DM]).then_inc(xc_ok, 1)

            def tanh(v, j):
                act.wait_ge(gu_ok, v + C + 1)
                act.wait_ge(hh_ok, v + C - 1)
                nc.scalar.activation(th[:, 1 - j], GU[1 - j][:, 0:INTER], ACT.Tanh, scale=0.5).then_inc(th_ok, 1)

            def row_b(m):
                act.wait_ge(row_ps[0], m + 1)
                act.wait_ge(dbu_ok, (DT - 1 - G1) * NS + m + 1)
                act.sem_inc(tick, 1)
                nc.scalar.copy(bc[:, bass.ds(m, 1), 0].rearrange("p a l -> p (a l)"), ROW[0][:]).then_inc(row_ok[0], 1)

            def light(g, Q):
                for m in range(LIGHT):
                    R, n = Q + m // 4, m // 3 * 2 + m % 3
                    copies(4 * R + m % 4, R, m % 4)
                    if m % 3 != 0:
                        decay(g + n // NS, n % NS, n % 2)
                    tanh(4 * R + m % 4, m % 2)

            def heavy(q, rows, after=None):
                for j4 in range(4):
                    copies(V_HEAVY + 4 * q + j4, V_HEAVY // 4 + q, j4)
                    if j4 == 1:
                        decay(GH, 2 * q + 1, 1)
                    elif j4 == 3:
                        decay(*(after or (GH, 2 * q + 2)), 0)
                    tanh(V_HEAVY + 4 * q + j4, j4 % 2)
                    if rows and j4 % 2:
                        row_b(2 * q + j4 // 2 - 2)

            act.wait_ge(scat, 16 * NT * K)
            decay(G1, 0, 0)
            with act.Fori(G1, GH) as g:
                light(g, (g - G1) * (LIGHT // 4))
            heavy(0, False)
            with act.Fori(1, QG - 1) as q:
                heavy(q, True)
            heavy(QG - 1, True, (GH + 1, 0))
            for m in range(NS - 2, NS):
                row_b(m)
            with act.Fori(GH + 1, G2) as g:
                light(g, (g - GH - 1) * (LIGHT // 4) + V_LAST // 4)
            decay(G2, 1, 1)
            for j in range(2):
                act.wait_ge(ye_ok, TILES + j + C + 1)
                if j == 0:
                    act.wait_ge(y_st[0], (TILES // 4) * 16 + 16)
                nc.scalar.copy(ysb[:, 0, j], YT[:, 0:DM]).then_inc(yc_ok, 1)
            act.wait_ge(c8_ok, NT * K)
            with act.Fori(1, NS // 4 + 1) as q:
                for j in range(2):
                    decay(G2, 2 * q + j, j)

            def output(t):
                nc.scalar.copy(x_sb[:, t], OUT[t]).then_inc(cb_out, 1)

            for t in range(NT - 1):
                for i in range(4):
                    s = 4 * (t + 2) + i + 2
                    if s < 2 * NS:
                        decay(G2 + s // NS, s % NS, s % 2)
                    if i == 1 and 1 <= t <= 4:
                        act.wait_ge(cb_ok, t * K + K)
                        output(t - 1)
                    for k in (2 * i, 2 * i + 1):
                        act.wait_ge(cb_ok, t * K + k + 1)
                        nc.scalar.activation(diag[:, k], ident[:], ACT.Copy, scale=c8[:, t, k:k + 1]).then_inc(dg_ok, 1)
            for t in range(4, NT - 1):
                act.wait_ge(o_ps, t - 3)
                output(t)

        @block.tensor
        def _(pe):
            pe.wait_ge(consts, CONSTS)
            for h in range(2):
                pe.wait_ge(ln, 2 * NT + 2 + (h + 1) * NT // 2)
                for k in range(KD):
                    for t in range(NT // 2):
                        mm = nc.tensor.transpose(PS[2 * h + k][:, t * P:(t + 1) * P],
                                                 x_sb[:, h * NT // 2 + t, k * P:(k + 1) * P], ident[:])
                    mm.then_inc(xt_ps, 1)
            pe.wait_ge(xt_ready, 4)
            pe.wait_ge(ld_gate, 16)
            for t in range(NT):
                for k in range(KD):
                    mm = nc.tensor.matmul(PS[4][:, t * E:(t + 1) * E], xT[:, k, t * P:(t + 1) * P], wgate[:, k],
                                          start=(k == 0), stop=(k == KD - 1))
            mm.then_inc(pe_r, 1)
            pe.wait_ge(ld_in, 16)

            def project_in(i):
                d, b = i // B, i % B
                if i >= 4:
                    pe.wait_ge(in_tap, i - 3)
                for k in range(KD):
                    mm = nc.tensor.matmul(PS[i % 4][:], win[:, k, d * P:(d + 1) * P], xT[:, k, b * L:(b + 1) * L],
                                          start=(k == 0), stop=(k == KD - 1))
                mm.then_inc(in_ps, 1)

            for i in range(4):
                project_in(i)
            pe.wait_ge(rt, RT_MASK)
            for t in range(NT):
                mm = nc.tensor.transpose(PS[5 + t // 4][0:E, t % 4 * P:(t % 4 + 1) * P], mask[:, t], ident[:])
            mm.then_inc(pe_r, 1)
            project_in(4)
            pe.wait_ge(rt, RT_NT)
            nc.tensor.matmul(PS[4][0:E, 0:1], tri[:], n_tile[:], start=True, stop=True).then_inc(pe_r, 1)
            project_in(5)
            pe.wait_ge(rt, RT_POS)
            for t in range(NT):
                mm = nc.tensor.transpose(PS[7][:, t * E:(t + 1) * E], cum[:, t * P:(t + 1) * P], ident[0:E, 0:E])
            mm.then_inc(pe_r, 1)
            pe.wait_ge(rt, RT_CMP)
            nc.tensor.matmul(PS[4][0:1, P:P + TILES], ones[0:E, 0:1], cmp, start=True, stop=True).then_inc(pe_r, 1)
            project_in(6)
            project_in(7)
            pe.wait_ge(ld_wx, 16)
            pe.wait_ge(in_tap, G)
            for k in range(DT):
                pe.wait_ge(u_ready, k + 1)
                for b in range(B):
                    mm = nc.tensor.matmul(PS[2 + b][0:3 * 2 * NS], wx[:, k, R:], u[:, b, k], start=(k == 0), stop=(k == DT - 1))
                    if k == DT - 1:
                        mm.then_inc(bc_ps, 1)
                for b in range(B):
                    mm = nc.tensor.matmul(PS[b][:], wx[:, k, 0:R], u[:, b, k], start=(k == 0), stop=(k == DT - 1))
                    if k == DT - 1:
                        mm.then_inc(dr_ps, 1)
            pe.wait_ge(ld_wdt, 16)
            pe.wait_ge(rt, RT_TILE)
            for g in range(G):
                pe.wait_ge(dr_ready, g // DT + 1)
                if g >= 4:
                    pe.wait_ge(dt_max, g - 3)
                nc.tensor.matmul(PS[4 + g % 4][:], wdt[:, g % DT * P:(g % DT + 1) * P], dtr[:, g // DT],
                                 start=True, stop=True).then_inc(dt_ps, 1)
            pe.wait_ge(dt_max, G)
            for i in range(G):
                d, b = i % DT, i // DT
                if i >= 4:
                    pe.wait_ge(z_ok, i - 3)
                for k in range(KD):
                    mm = nc.tensor.matmul(PS[4 + d][:], win[:, k, DI + d * P:DI + (d + 1) * P], xT[:, k, b * L:(b + 1) * L],
                                          start=(k == 0), stop=(k == KD - 1))
                mm.then_inc(z_ps, 1)
            for s_ in (gu_ok, acc_ok, ye_ok):
                pe.sem_inc(s_, C)
            pe.sem_inc(cb_ok, K)
            for c in range(2):
                pe.sem_inc(row_ok[c], 1)

            def sum_states(g, n, j, first):
                pe.wait_ge(hc_ok, g * NS + n + C + 1)
                if first:
                    pe.wait_ge(y_out, g + 1)
                nc.tensor.matmul(Y_ACC[:], ident[:], hc[:, j], start=first, stop=True, skip_group_check=True).then_inc(acc_ok, 1)

            for n in range(NS - 2):
                sum_states(0, n, n % 2, n == 0)
            pe.wait_ge(z_ok, G)

            def tile_slot(O, i):
                v, j = 8 * O + i, i % 2
                down(v, (i + 5) % 8)
                if j == 0:
                    pe.wait_ge(xg_ld[i // 2], O * 16 + 16)
                pe.wait_ge(xc_ok, v + C)
                for k in range(KD):
                    mm = nc.tensor.transpose(XT[:, k * P:(k + 1) * P], x_buf[i // 2][:, j, k * P:(k + 1) * P], ident[:])
                mm.then_inc(t_ok, 1)
                w = (i + 7) % 8
                pe.wait_ge(w_ld[w], O * 16 + 16)
                pe.wait_ge(hh_ok, v + C - 1)
                for half in range(2):
                    for k in range(KD):
                        mm = nc.tensor.matmul(GU[1 - j][:, half * P:(half + 1) * P],
                                              w_buf[w][:, k * 2 * P + half * P:k * 2 * P + (half + 1) * P],
                                              xTs[:, 1 - j, k * P:(k + 1) * P], start=(k == 0), stop=(k == KD - 1))
                mm.then_inc(gu_ok, 1)

            def down(v, w):
                pe.wait_ge(hh_ok, v - 1 + C)
                pe.wait_ge(yc_ok, v + C)
                nc.tensor.matmul(YT[:, 0:DM], hh[:, w % 4], w_buf[w][:, WGU:], start=True, stop=True).then_inc(ye_ok, 1)

            def sum_pair(r, g=None):
                pe.wait_ge(hp_ok, r + 2)
                if g is not None:
                    pe.wait_ge(y_out, g + 1)
                nc.tensor.matmul(Y_ACC[:], ident[:], hp[:], start=(g is not None), stop=True,
                                 skip_group_check=True).then_inc(acc_ok, 2)

            def row(c, m):
                pe.wait_ge(row_ok[c], m + 1)
                nc.tensor.matmul(ROW[c][:], pick[:, bass.ds(c * NS + m, 1)].broadcast_to([3 * 2 * NS, P]), parts[:],
                                 start=True, stop=True).then_inc(row_ps[c], 1)

            def light(g, O):
                for m in range(LIGHT):
                    tile_slot(O + m // 8, m % 8)
                    if m % 3 == 2:
                        sum_pair((g - G1) * QG + m // 3 - 1, g if m // 3 == 1 else None)

            def heavy(o, begin):
                for i in range(8):
                    q = 2 * o + i // 4
                    tile_slot(V_HEAVY // 8 + o, i)
                    if i % 4 == 2:
                        sum_pair((GH - G1) * QG + q - 1, GH if begin and i > 4 else None)
                    if i > 3 or not begin:
                        row(i % 2, 2 * q + i % 4 // 2 - 2)

            with pe.Fori(G1, GH) as g:
                light(g, (g - G1) * (LIGHT // 8))
            heavy(0, True)
            with pe.Fori(1, QG // 2) as o:
                heavy(o, False)
            for m in range(NS - 2, NS):
                row(0, m)
                row(1, m)
            with pe.Fori(GH + 1, G2) as g:
                light(g, (g - GH - 1) * (LIGHT // 8) + V_LAST // 8)
            for j in range(2):
                down(TILES + j, 5 + j)
            sum_pair((G2 - G1) * QG - 1)
            pe.wait_ge(xc_ok, TILES + C)

            def combine(t, ks):
                if ks[0] == 0:
                    nc.tensor.matmul(OUT[t], ident[:], x_sb[:, t], start=False, stop=False)
                    pe.wait_ge(g_ld[t % 4], (t // 4 + 1) * 16 * K)
                for k in ks:
                    pe.wait_ge(dg_ok, t * K + k + 1)
                    nc.tensor.matmul(OUT[t], diag[:, k], rows[t % 4][:, k], start=False,
                                     stop=(k == K - 1 and t < 4)).then_inc(cb_ok, 1)

            def project_out(t, k):
                b, c = t // (L // P), t % (L // P)
                return nc.tensor.matmul(OUT[t], u[:, b, k, c * P:(c + 1) * P], wout[:, k], start=(k == 0),
                                        stop=(k == DT - 1 and t >= 4))

            pe.wait_ge(ld_wout, 16)
            pe.wait_ge(yz_ok, DT)
            pe.wait_ge(hh_ok, TILES + C)
            for n in range(NS // 2):
                sum_states(G2, n, n % 2, n == 0)
                if n == 6:
                    pe.wait_ge(yc_ok, TILES + 2 + C)
                for k in (n % 2 * 2, n % 2 * 2 + 1):
                    project_out(n // 2, k)
            pe.wait_ge(ld_res, 16)
            for s in range(NS // 2, 2 * NS):
                n, i = s % NS, s % 4
                sum_states(G2 + s // NS, n, n % 2, n == 0)
                combine(s // 4 - 2, (2 * i, 2 * i + 1))
                if s in PROJ:
                    t, k = PROJ[s]
                    pe.wait_ge(yz_ok, DT + k + 1)
                    if k == 0:
                        if t >= 6:
                            pe.wait_ge(cb_out, t - 5)
                        else:
                            pe.wait_ge(row_ok[t - 4], NS + 1)
                    project_out(t, k)
            combine(NT - 2, range(K))
            pe.wait_ge(yz_ok, G)
            for t in range(4, NT):
                project_out(t, DT - 1).then_inc(o_ps, 1)


def kernel(**inputs):
    import numpy as np
    import concourse.bacc as bacc
    from concourse.bass_utils import run_bass_kernel_spmd as run

    a = {k: np.asarray(v) for k, v in inputs.items()}
    x = a["L0_attn_hidden_states"].reshape(T, DM)
    par = np.concatenate([a["L0_attn_conv_w"], a["L0_attn_conv_b"][:, None], a["L0_attn_dt_proj_b"][:, None],
                          a["L0_attn_D"][:, None], a["L0_attn_A_log"]], axis=1)
    w_x = a["L0_attn_x_proj_w"].T
    w13 = a["L0_ffn_w13"].transpose(0, 2, 1)
    w13 = w13.reshape(E, KD, P, 2 * INTER).transpose(0, 2, 1, 3).reshape(E, P, KD * 2 * INTER)
    w_moe = np.concatenate([w13, a["L0_ffn_w2"].transpose(0, 2, 1)], axis=2)
    arrays = {
        "x": x, "w_in": a["L0_attn_in_proj_w"].T, "par": par, "w_x": np.concatenate([w_x[:, 0:R]] + 3 * [w_x[:, R:]], axis=1),
        "w_dt": a["L0_attn_dt_proj_w"].T, "w_out": a["L0_attn_out_proj_w"].T, "w_gate": a["L0_ffn_gate_w"].T,
        "w_moe": w_moe,
    }
    arrays = {k: np.ascontiguousarray(v) for k, v in arrays.items()}
    nc = bacc.Bacc("TRN2", target_bir_lowering=False, num_devices=1)
    args = [nc.dram_tensor(k, v.shape, F32, kind="ExternalInput").ap() for k, v in arrays.items()]
    out = nc.dram_tensor("out", (T, DM), F32, kind="ExternalOutput").ap()
    bc_dram = nc.dram_tensor("bc_dram", (2 * NS, L), F32).ap()
    slot_x = nc.dram_tensor("slot_x", (TILES * P, DM), F32).ap()
    slot_y = nc.dram_tensor("slot_y", ((TILES + 2) * P, DM), F32).ap()
    program(nc, *args, out, bc_dram, slot_x, slot_y)
    r = run(nc, [arrays], core_ids=[0])
    return r.results[0]["out"].reshape(B, L, DM)
```
